# Optimizing a Trainium2 kernel written in Bass

```python
import numpy as np
import jax
import jax.numpy as jnp

def _softmax(x, axis=-1):
    return jax.nn.softmax(x, axis=axis)

def _gelu(x):
    return jax.nn.gelu(x, approximate=True)

def _silu(x):
    return jax.nn.silu(x)

def _sigmoid(x):
    return jax.nn.sigmoid(x)

def _layernorm(x, axis=-1, eps=1e-05):
    m = jnp.mean(x, axis=axis, keepdims=True)
    v = jnp.var(x, axis=axis, keepdims=True)
    return (x - m) / jnp.sqrt(v + eps)

def _scatter_add(tgt, idx, src, axis=0):
    return tgt.at[idx].add(src)

def _segment_sum(src, seg, n):
    return jax.ops.segment_sum(src, seg, n)
kernel_name = 'mk_seq_postln_d1_jaxref_r8_7c5d57'

def setup_inputs(seed: int=0):
    np.random.seed(seed)
    _w = jnp.asarray

    def _L0_attn_setup():
        import jax, jax.numpy as jnp
        import numpy as np
        import math
        INPUT_SIZE = 128
        HIDDEN = 128
        SEQ_LEN = 32
        BATCH = 128

        def _lstm(input_seq, w, u, bias):
            H = u.shape[0]
            B = input_seq.shape[1]
            x_proj = jnp.einsum('sbi,ih->sbh', input_seq, w) + bias

            def step(carry, xp_t):
                h_prev, c_prev = carry
                g = xp_t + h_prev @ u
                gates = jax.nn.sigmoid(g[:, :3 * H])
                c_cand = jnp.tanh(g[:, 3 * H:])
                ig, fg, og = (gates[:, :H], gates[:, H:2 * H], gates[:, 2 * H:])
                c = fg * c_prev + ig * c_cand
                h = og * jnp.tanh(c)
                return ((h, c), h)
            init = (jnp.zeros((B, H), dtype=input_seq.dtype), jnp.zeros((B, H), dtype=input_seq.dtype))
            _, hs = jax.lax.scan(step, init, x_proj)
            return hs
        key = jax.random.key(seed)
        k1, k2, k3, k4 = jax.random.split(key, 4)
        stddev = 1.0 / math.sqrt(HIDDEN)
        input_seq = jax.random.normal(k1, (SEQ_LEN, BATCH, INPUT_SIZE), dtype=jnp.float32)
        w = jax.random.uniform(k2, (INPUT_SIZE, 4 * HIDDEN), minval=-stddev, maxval=stddev, dtype=jnp.float32)
        u = jax.random.uniform(k3, (HIDDEN, 4 * HIDDEN), minval=-stddev, maxval=stddev, dtype=jnp.float32)
        bias = jax.random.uniform(k4, (4 * HIDDEN,), minval=-stddev, maxval=stddev, dtype=jnp.float32)
        return {'input_seq': input_seq, 'w': w, 'u': u, 'bias': bias}
    _L0_attn_in = _L0_attn_setup()

    def _L0_ffn_setup():
        import jax, jax.numpy as jnp
        import numpy as np
        B, L, M = (4, 256, 128)
        G, E = (8, 8)
        CAP_FACTOR = 2.0

        def _ffn_size(m, widening=8.0):
            f = int(widening * m) * 2 // 3
            return f + (8 - f) % 8
        H = _ffn_size(M)

        def _gating_top2(logits, C):
            Gd, Sd, Ed = logits.shape
            raw = jax.nn.softmax(logits, axis=-1)
            idx1 = jnp.argmax(raw, axis=-1)
            m1 = jax.nn.one_hot(idx1, Ed, dtype=logits.dtype)
            gate1 = jnp.sum(raw * m1, axis=-1)
            rest = raw * (1.0 - m1)
            idx2 = jnp.argmax(rest, axis=-1)
            m2 = jax.nn.one_hot(idx2, Ed, dtype=logits.dtype)
            gate2 = jnp.sum(rest * m2, axis=-1)
            p1 = jnp.cumsum(m1, axis=-2) - m1
            m1 = m1 * (p1 < C).astype(m1.dtype)
            p1 = jnp.sum(p1 * m1, axis=-1)
            m1_flat = jnp.sum(m1, axis=-1)
            m1_count = jnp.sum(m1, axis=-2)
            p2 = jnp.cumsum(m2, axis=-2) - m2 + m1_count[:, None, :]
            m2 = m2 * (p2 < C).astype(m2.dtype)
            p2 = jnp.sum(p2 * m2, axis=-1)
            m2_flat = jnp.sum(m2, axis=-1)
            gate1 = gate1 * m1_flat
            gate2 = gate2 * m2_flat
            c1 = (gate1[..., None] * jax.nn.one_hot(idx1, Ed, dtype=jnp.float32))[..., None] * jax.nn.one_hot(p1.astype(jnp.int32), C, dtype=jnp.float32)[:, :, None, :]
            c2 = (gate2[..., None] * jax.nn.one_hot(idx2, Ed, dtype=jnp.float32))[..., None] * jax.nn.one_hot(p2.astype(jnp.int32), C, dtype=jnp.float32)[:, :, None, :]
            combine = (c1 + c2).astype(logits.dtype)
            dispatch = (combine != 0).astype(logits.dtype)
            return (dispatch, combine)
        key = jax.random.key(seed)
        k0, k1, k2, k3, k4 = jax.random.split(key, 5)
        return {'inputs': jax.random.normal(k0, (B, L, M), jnp.float32), 'router_w': jax.random.normal(k1, (M, E), jnp.float32) * 0.02, 'w0_kernel': jax.random.normal(k2, (E, M, H), jnp.float32) * 0.02, 'w1_kernel': jax.random.normal(k3, (E, M, H), jnp.float32) * 0.02, 'wo_kernel': jax.random.normal(k4, (E, H, M), jnp.float32) * 0.02}
    _L0_ffn_in = _L0_ffn_setup()
    _d = {'L0_attn_input_seq': _L0_attn_in['input_seq'], 'L0_attn_w': _L0_attn_in['w'], 'L0_attn_u': _L0_attn_in['u'], 'L0_attn_bias': _L0_attn_in['bias'], 'L0_ffn_router_w': _L0_ffn_in['router_w'], 'L0_ffn_w0_kernel': _L0_ffn_in['w0_kernel'], 'L0_ffn_w1_kernel': _L0_ffn_in['w1_kernel'], 'L0_ffn_wo_kernel': _L0_ffn_in['wo_kernel']}
    _x0 = _d['L0_attn_input_seq']
    _d['L0_attn_input_seq'] = jax.random.normal(jax.random.fold_in(jax.random.key(seed), 1), (8, 512, 128), dtype=_x0.dtype)
    del _x0
    return _d

def reference(L0_attn_input_seq, L0_attn_w, L0_attn_u, L0_attn_bias, L0_ffn_router_w, L0_ffn_w0_kernel, L0_ffn_w1_kernel, L0_ffn_wo_kernel):

    def _L0_attn_ref(input_seq, w, u, bias):
        import jax, jax.numpy as jnp
        import numpy as np
        import math
        INPUT_SIZE = 128
        HIDDEN = 128
        SEQ_LEN = 32
        BATCH = 128

        def _lstm(input_seq, w, u, bias):
            H = u.shape[0]
            B = input_seq.shape[1]
            x_proj = jnp.einsum('sbi,ih->sbh', input_seq, w) + bias

            def step(carry, xp_t):
                h_prev, c_prev = carry
                g = xp_t + h_prev @ u
                gates = jax.nn.sigmoid(g[:, :3 * H])
                c_cand = jnp.tanh(g[:, 3 * H:])
                ig, fg, og = (gates[:, :H], gates[:, H:2 * H], gates[:, 2 * H:])
                c = fg * c_prev + ig * c_cand
                h = og * jnp.tanh(c)
                return ((h, c), h)
            init = (jnp.zeros((B, H), dtype=input_seq.dtype), jnp.zeros((B, H), dtype=input_seq.dtype))
            _, hs = jax.lax.scan(step, init, x_proj)
            return hs
        return _lstm(input_seq, w, u, bias)

    def _L0_ffn_ref(inputs, router_w, w0_kernel, w1_kernel, wo_kernel):
        import jax, jax.numpy as jnp
        import numpy as np
        B, L, M = (4, 256, 128)
        G, E = (8, 8)
        CAP_FACTOR = 2.0

        def _ffn_size(m, widening=8.0):
            f = int(widening * m) * 2 // 3
            return f + (8 - f) % 8
        H = _ffn_size(M)

        def _gating_top2(logits, C):
            Gd, Sd, Ed = logits.shape
            raw = jax.nn.softmax(logits, axis=-1)
            idx1 = jnp.argmax(raw, axis=-1)
            m1 = jax.nn.one_hot(idx1, Ed, dtype=logits.dtype)
            gate1 = jnp.sum(raw * m1, axis=-1)
            rest = raw * (1.0 - m1)
            idx2 = jnp.argmax(rest, axis=-1)
            m2 = jax.nn.one_hot(idx2, Ed, dtype=logits.dtype)
            gate2 = jnp.sum(rest * m2, axis=-1)
            p1 = jnp.cumsum(m1, axis=-2) - m1
            m1 = m1 * (p1 < C).astype(m1.dtype)
            p1 = jnp.sum(p1 * m1, axis=-1)
            m1_flat = jnp.sum(m1, axis=-1)
            m1_count = jnp.sum(m1, axis=-2)
            p2 = jnp.cumsum(m2, axis=-2) - m2 + m1_count[:, None, :]
            m2 = m2 * (p2 < C).astype(m2.dtype)
            p2 = jnp.sum(p2 * m2, axis=-1)
            m2_flat = jnp.sum(m2, axis=-1)
            gate1 = gate1 * m1_flat
            gate2 = gate2 * m2_flat
            c1 = (gate1[..., None] * jax.nn.one_hot(idx1, Ed, dtype=jnp.float32))[..., None] * jax.nn.one_hot(p1.astype(jnp.int32), C, dtype=jnp.float32)[:, :, None, :]
            c2 = (gate2[..., None] * jax.nn.one_hot(idx2, Ed, dtype=jnp.float32))[..., None] * jax.nn.one_hot(p2.astype(jnp.int32), C, dtype=jnp.float32)[:, :, None, :]
            combine = (c1 + c2).astype(logits.dtype)
            dispatch = (combine != 0).astype(logits.dtype)
            return (dispatch, combine)
        Bb, Ll, Mm = inputs.shape
        S = Bb * Ll // G
        x = inputs.reshape(G, S, Mm)
        logits = jnp.einsum('GSM,ME->GSE', x, router_w)
        cap = int(CAP_FACTOR * S / E)
        C = (cap + 3) // 4 * 4
        dispatch, combine = _gating_top2(logits, C)
        expert_inputs = jnp.einsum('GSEC,GSM->EGCM', dispatch, x)
        layer_w0 = jnp.einsum('EGCM,EMH->EGCH', expert_inputs, w0_kernel)
        layer_w1 = jnp.einsum('EGCM,EMH->EGCH', expert_inputs, w1_kernel)
        hidden = jax.nn.gelu(layer_w0, approximate=True) * layer_w1
        expert_outputs = jnp.einsum('EGCH,EHM->EGCM', hidden, wo_kernel)
        out = jnp.einsum('EGCM,GSEC->GSM', expert_outputs, combine)
        return out.reshape(Bb, Ll, Mm)
    x = L0_attn_input_seq
    x = _layernorm(x + _L0_attn_ref(x, L0_attn_w, L0_attn_u, L0_attn_bias), axis=-1)
    x = _layernorm(x + _L0_ffn_ref(x, L0_ffn_router_w, L0_ffn_w0_kernel, L0_ffn_w1_kernel, L0_ffn_wo_kernel), axis=-1)
    return x

_drawn_inputs = setup_inputs


def setup_inputs(seed=0):
    import zlib

    import numpy as np

    out = dict(_drawn_inputs(seed))
    spreads = {}
    factors = {'L0_attn_bias': 3.097,
     'L0_ffn_router_w': 8.0,
     'L0_ffn_w0_kernel': 8.0,
     'L0_ffn_w1_kernel': 8.0,
     'L0_ffn_wo_kernel': 8.0}
    for name, (base, spread) in spreads.items():
        noise = np.random.default_rng([zlib.crc32(name.encode()), seed]).standard_normal(out[name].shape)
        drawn = base * np.exp(spread * noise) if base else spread * noise
        out[name] = jnp.asarray(drawn.astype(out[name].dtype))
    for name, factor in factors.items():
        out[name] = (out[name] * factor).astype(out[name].dtype)
    return out
```

```python
from contextlib import ExitStack

import concourse.bass as bass
from concourse import mybir

F32 = mybir.dt.float32
F32R = mybir.dt.float32r
BF16 = mybir.dt.bfloat16
U32 = mybir.dt.uint32
I32 = mybir.dt.int32
ALU = mybir.AluOpType
ACT = mybir.ActivationFunctionType
AX = mybir.AxisListType


def build(nc, x_in, w_in, u_in, b_in, rw_in, w0_in, w1_in, wo_in, out):
    S, N, D = x_in.shape
    P = 128
    assert D == P
    E, _, H = w0_in.shape
    T = N // P
    C = (int(2.0 * N / E) + 3) // 4 * 4
    assert C == P
    EPS = 1e-5
    FULL = H // P
    TAIL = H - FULL * P
    HALF = S // 2
    ROW = D + 1 + E
    FAR = float(1 << 20)
    GB = 2
    BT = GB * T
    NB = S // GB
    W1C, WTC, WOC = FULL * P, 2 * FULL * P, (2 * FULL + 1) * P
    WCOLS = WOC + (FULL + 1) * P
    NCH = FULL + 1
    RT = 11
    RS = 14
    RH = 3

    gate_order = [1, 0, 3, 2]

    with ExitStack() as ctx:
        def sb(name, shape, dt=F32):
            return ctx.enter_context(nc.sbuf_tensor(name, shape, dt))

        def bank(name):
            return ctx.enter_context(nc.psum_tensor(name, [P, 512], F32))

        def sem(name):
            return ctx.enter_context(nc.semaphore(name))

        slots = nc.dram_tensor("slots", [S * E * C, ROW], F32, kind="Internal").ap()
        tokens = nc.dram_tensor("tokens", [S * N, D], F32, kind="Internal").ap()

        ident = sb("ident", [P, P])
        ones = sb("ones", [P, P])
        ones_b = sb("ones_b", [P, P], BF16)
        before = sb("before", [P, P], BF16)
        zero_rows = sb("zero_rows", [P, 2 * E * ROW])
        w_raw = sb("w_raw", [P, 4 * D])
        u_raw = sb("u_raw", [P, 4 * D])
        w_hi, w_lo = sb("w_hi", [P, 4 * D], F32R), sb("w_lo", [P, 4 * D], F32R)
        u_half = sb("u_half", [P, 4 * D])
        u_hi, u_lo = sb("u_hi", [P, 4 * D], F32R), sb("u_lo", [P, 4 * D], F32R)
        bias = sb("bias", [P, 4])
        bias_g = sb("bias_g", [P, 4])
        rw = sb("rw", [P, E])
        x_sb = [sb(f"x{s}", [P, T, D]) for s in range(S)]
        xt_hi = [sb(f"xt_hi{q}", [P, N], F32R) for q in range(2)]
        xt_lo = [sb(f"xt_lo{q}", [P, N], F32R) for q in range(2)]
        act_g = [sb(f"act_g{k}", [P, N]) for k in range(4)]
        term_f, term_i = sb("term_f", [P, N]), sb("term_i", [P, N])
        cell2 = sb("cell2", [P, N])
        tanh_c = sb("tanh_c", [P, N])
        h2 = sb("h2", [P, N])
        h_hi, h_lo = sb("h_hi", [P, N], F32R), sb("h_lo", [P, N], F32R)
        y_sb = sb("y_sb", [P, T, D])
        stats = sb("stats", [P, T, 6])
        moments = sb("moments", [P, T, 2])
        rstd = sb("rstd", [P, T])
        var_eps, newton = sb("var_eps", [P, T]), sb("newton", [P, T])
        rows = sb("rows", [P, S * T, ROW])
        xnt = sb("xnt", [P, N])
        toknum_i = sb("toknum_i", [P, S * T], I32)
        slot0_i = sb("slot0_i", [P, BT, E], I32)
        rev_i = sb("rev_i", [P, BT, E], I32)
        slot0 = sb("slot0", [P, BT, E])
        rev = sb("rev", [P, BT, E])
        lg = sb("lg", [P, BT, E])
        ex = sb("ex", [P, BT, E])
        raw = sb("raw", [P, BT, E])
        eq = sb("eq", [P, BT, E])
        picked = sb("picked", [P, BT, E])
        rest = sb("rest", [P, BT, E])
        col, rsum = sb("col", [P, BT]), sb("rsum", [P, BT])
        gates = sb("gates", [P, 2, BT])
        chosen = sb("chosen", [P, 2, BT, E], BF16)
        cnt = sb("cnt", [P, GB, E])
        place = sb("place", [P, 2, BT, E])
        over = sb("over", [P, 2, BT, E])
        slot_f = sb("slot_f", [P, 2, BT])
        void = sb("void", [P, 2, BT])
        slot_ix = [sb(f"slot_ix{b}", [P, 2 * BT], U32) for b in range(NB)]
        e_raw = [sb(f"e_raw{q}", [P, WCOLS]) for q in range(2)]
        e_hi = [sb(f"e_hi{q}", [P, WCOLS], F32R) for q in range(2)]
        e_lo = [sb(f"e_lo{q}", [P, WCOLS], F32R) for q in range(2)]
        xd = [sb(f"xd{r}", [P, HALF, ROW]) for r in range(4)]
        xdt_hi = [sb(f"xdt_hi{q}", [P, HALF * C], F32R) for q in range(2)]
        xdt_lo = [sb(f"xdt_lo{q}", [P, HALF * C], F32R) for q in range(2)]
        act0 = [sb(f"act0_{r}", [P, 512]) for r in range(RH)]
        hid = [sb(f"hid{r}", [P, 512]) for r in range(RH)]
        hid_hi = [sb(f"hid_hi{r}", [P, 512], F32R) for r in range(RH)]
        hid_lo = [sb(f"hid_lo{r}", [P, 512], F32R) for r in range(RH)]
        yt = sb("yt", [P, HALF * C])
        contrib = [sb(f"contrib{q}", [P, HALF, D]) for q in range(2)]
        token_ix = [sb(f"token_ix{q}", [P, HALF], U32) for q in range(2)]
        fin = x_sb
        fin_stats = sb("fin_stats", [P, S, T, 6])
        fin_mom = sb("fin_mom", [P, S, T, 2])
        fin_rstd = sb("fin_rstd", [P, S, T])

        big = [bank(f"big{k}") for k in range(4)]
        b_xt, b_ht, b_xnt, b_rt = bank("b_xt"), bank("b_ht"), bank("b_xnt"), bank("b_rt")
        lg_ps = b_rt[:, 0:BT * E].rearrange("p (t e) -> p t e", e=E)
        pl_ps = b_rt[:, 128:128 + 2 * BT * E].rearrange("p (c t e) -> p c t e", c=2, e=E)
        cn_ps = b_rt[:, 256:256 + GB * E].rearrange("p (g e) -> p g e", e=E)
        b_y = [b_ht, b_xnt]

        consts_in = sem("consts_in")
        x_in_s = [sem(f"x_in{s}") for s in range(S)]
        zeros_made, zeros_out = sem("zeros_made"), sem("zeros_out")
        pool_consts, dve_consts, act_consts = sem("pool_consts"), sem("dve_consts"), sem("act_consts")
        xt_ready, xhi_ready, xlo_ready = sem("xt_ready"), sem("xhi_ready"), sem("xlo_ready")
        gate_ready, gate_read = sem("gate_ready"), sem("gate_read")
        terms_ready, cell_ready, tanh_ready = sem("terms_ready"), sem("cell_ready"), sem("tanh_ready")
        h_ready, hhi_ready, hlo_ready, ht_ready = sem("h_ready"), sem("hhi_ready"), sem("hlo_ready"), sem("ht_ready")
        y_ready, stats_ready, mom_ready, root_step = sem("y_ready"), sem("stats_ready"), sem("mom_ready"), sem("root_step")
        xn_ready, xnt_ready, xnt_copied = sem("xn_ready"), sem("xnt_ready"), sem("xnt_copied")
        logits_ready, route_step, exp_ready = sem("logits_ready"), sem("route_step"), sem("exp_ready")
        chosen_ready, places_ready, slots_ready = sem("chosen_ready"), sem("places_ready"), sem("slots_ready")
        resid_out = sem("resid_out")
        picked_ready, gatevec_ready = sem("picked_ready"), sem("gatevec_ready")
        slot_step, slotf_ready = sem("slot_step"), sem("slotf_ready")
        routed = [sem(f"routed{b}") for b in range(NB)]
        raw_in = [sem(f"raw_in{q}") for q in range(2)]
        raw_clear, ehi_ready, elo_ready = sem("raw_clear"), sem("ehi_ready"), sem("elo_ready")
        xd_in = [sem(f"xd_in{r}") for r in range(4)]
        xdt_ready, xdhi_ready, xdlo_ready = sem("xdt_ready"), sem("xdhi_ready"), sem("xdlo_ready")
        pre_ready, gelu_ready, hid_ready = sem("pre_ready"), sem("gelu_ready"), sem("hid_ready")
        hidhi_ready, hidlo_ready, chunk_used = sem("hidhi_ready"), sem("hidlo_ready"), sem("chunk_used")
        y_done, yt_copied, eo_ready = sem("y_done"), sem("yt_copied"), sem("eo_ready")
        contrib_ready, added = sem("contrib_ready"), [sem(f"added{q}") for q in range(2)]
        fin_in = [sem(f"fin_in{g}") for g in range(S)]
        fstats_ready, fmom_ready, fin_ready = sem("fstats"), sem("fmom"), sem("fin_ready")
        out_done = sem("out_done")

        NU = 2 * E

        def unit(u):
            j, r = divmod(u, 4)
            return 2 * j + r % 2, r // 2

        def expert_done(e):
            return 4 * (e // 2) + 3 + e % 2

        block = ctx.enter_context(nc.Block())

        @block.sync
        def _(sp):
            def load_x(s):
                sp.dma_start(x_sb[s][:, :, :], x_in[s].rearrange("(t p) i -> p t i", p=P)).then_inc(x_in_s[s], 16)

            def load_expert(e):
                q = e % 2
                if e < 2:
                    sp.wait_ge(raw_clear, 2)
                else:
                    sp.wait_ge(elo_ready, e - 1)
                r = e_raw[q]
                for k, (src, dst) in enumerate([
                        (w0_in[e, :, 0:FULL * P], r[:, 0:W1C]), (w1_in[e, :, 0:FULL * P], r[:, W1C:WTC]),
                        (w0_in[e, :, FULL * P:H], r[:, WTC:WTC + TAIL]),
                        (w1_in[e, :, FULL * P:H], r[:, WTC + 64:WTC + 64 + TAIL]),
                        (wo_in[e, 0:FULL * P, :].rearrange("(k p) m -> p k m", p=P),
                         r[:, WOC:WOC + FULL * P].rearrange("p (k m) -> p k m", k=FULL)),
                        (wo_in[e, FULL * P:H, :], r[0:TAIL, WOC + FULL * P:WCOLS])]):
                    sp.dma_start(dst, src).then_inc(raw_in[q], 16)

            load_x(0)
            sp.dma_start(w_raw[:, :], w_in[:, :]).then_inc(consts_in, 16)
            sp.dma_start(bias[:, :], b_in.rearrange("(g h) -> h g", g=4), allow_slow_non_contiguous=True).then_inc(consts_in, 16)
            sp.dma_start(u_raw[:, :], u_in[:, :]).then_inc(consts_in, 16)
            sp.dma_start(rw[:, :], rw_in[:, :]).then_inc(consts_in, 16)
            for s in range(1, S):
                load_x(s)
            sp.wait_ge(zeros_made, 1)
            for b in range(S // 2):
                n = 2 * E * C
                sp.dma_start(slots[b * n:(b + 1) * n, :].rearrange("(p r) f -> p (r f)", p=P), zero_rows[:, :]).then_inc(zeros_out, 16)
            load_expert(0)
            load_expert(1)
            for s in range(S):
                sp.wait_ge(xn_ready, T * (s + 1))
                sp.dma_start(tokens[s * N:(s + 1) * N, :].rearrange("(t p) d -> p t d", p=P),
                             rows[:, s * T:(s + 1) * T, 0:D]).then_inc(resid_out, 16)

            def load_xd(u):
                e, half = unit(u)
                r = u % 4
                for b in range(NB // 2 * half, NB // 2 * (half + 1)):
                    sp.wait_ge(routed[b], 16 * 2 * BT)
                if u >= 4:
                    sp.wait_ge(xdt_ready, u - 3)
                    sp.wait_ge(contrib_ready, 2 * (u - 3))
                sp.dma_start(xd[r][:, :, :], slots.rearrange("(g e c) f -> e c g f", g=S, e=E)[
                    e, :, HALF * half:HALF * (half + 1), :]).then_inc(xd_in[r], 16)

            load_xd(0)
            load_xd(1)
            for u in range(NU):
                if u + 2 < NU:
                    load_xd(u + 2)
                if u % 4 == 0 and u > 0:
                    load_expert(u // 2)
                    load_expert(u // 2 + 1)

            for g in range(S):
                u = NU - 3 if g < HALF else NU - 1
                for q in range(2):
                    sp.wait_ge(added[q], 16 * HALF * ((u - q + 1) // 2 + (1 if (u - q) % 2 == 0 and q == 0 else 0)) if False else 16 * HALF * (((u if u % 2 == q else u - 1) // 2) + 1))
                sp.dma_start(fin[g][:, :, :], tokens[g * N:(g + 1) * N, :].rearrange("(t p) d -> p t d", p=P)).then_inc(fin_in[g], 16)
            for g in range(S):
                sp.wait_ge(fin_ready, T * (g + 1))
                sp.dma_start(out[g].rearrange("(t p) d -> p t d", p=P), fin[g][:, :, :]).then_inc(out_done, 16)
            sp.wait_ge(out_done, 16 * S)

        @block.gpsimd
        def _(pool):
            pool.memset(zero_rows[:, :], 0.0).then_inc(zeros_made, 1)
            pool.memset(ones[:, :], 1.0).then_inc(pool_consts, 1)
            pool.wait_ge(pool_consts, 1)
            pool.affine_select(ident[:, :], ones[:, :], [[1, P]], ALU.is_equal, 0.0, base=0, channel_multiplier=-1).then_inc(pool_consts, 1)
            pool.memset(ones_b[:, :], 1.0).then_inc(pool_consts, 1)
            pool.wait_ge(pool_consts, 3)
            pool.affine_select(before[:, :], ones_b[:, :], [[1, P]], ALU.is_gt, 0.0, base=0, channel_multiplier=-1).then_inc(pool_consts, 1)
            pool.iota(toknum_i[:, :], [[P, S * T]], base=0, channel_multiplier=1).then_inc(pool_consts, 1)
            pool.iota(slot0_i[:, :, :], [[E * C, GB], [0, T], [C, E]], base=0, channel_multiplier=0).then_inc(pool_consts, 1)
            pool.iota(rev_i[:, :, :], [[0, BT], [-1, E]], base=E, channel_multiplier=0).then_inc(pool_consts, 1)
            for q in range(2):
                pool.memset(e_raw[q][:, WTC:WCOLS], 0.0).then_inc(raw_clear, 1)

            def split_expert(e):
                q = e % 2
                pool.wait_ge(raw_in[q], 96 * (e // 2 + 1))
                if e >= 2:
                    pool.wait_ge(chunk_used, NCH * expert_done(e - 2))
                pool.tensor_copy(e_hi[q][:, :], e_raw[q][:, :]).then_inc(ehi_ready, 1)
                pool.wait_ge(ehi_ready, e + 1)
                pool.tensor_tensor(e_lo[q][:, :], e_raw[q][:, :], e_hi[q][:, :], ALU.subtract).then_inc(elo_ready, 1)

            split_expert(0)
            split_expert(1)
            pool.wait_ge(zeros_out, 16 * (S // 2))
            for b in range(NB):
                pool.wait_ge(slots_ready, b + 1)
                for t in range(BT):
                    for c in range(2):
                        pool.indirect_dma_start(
                            slots, bass.IndirectOffsetOnAxis(ap=slot_ix[b][:, c * BT + t:c * BT + t + 1], axis=0),
                            rows[:, b * BT + t, :], None, bounds_check=S * E * C - 1, oob_is_err=False).then_inc(routed[b], 16)

            pool.wait_ge(resid_out, 16 * S)
            for u in range(NU):
                e, half = unit(u)
                if u % 4 >= 2 and e + 2 < E:
                    split_expert(e + 2)
                pool.wait_ge(contrib_ready, 2 * (u + 1))
                if u >= 1:
                    pool.wait_ge(added[(u - 1) % 2], 16 * HALF * ((u - 1) // 2 + 1))
                for k in range(HALF):
                    pool.indirect_dma_start(
                        tokens, bass.IndirectOffsetOnAxis(ap=token_ix[u % 2][:, k:k + 1], axis=0),
                        contrib[u % 2][:, k, :], None, bounds_check=S * N - 1, oob_is_err=False,
                        compute_op=ALU.add).then_inc(added[u % 2], 16)

        @block.tensor
        def _(pe):
            def turn_x(s):
                pe.wait_ge(x_in_s[s], 16)
                if s >= 1:
                    pe.wait_ge(xhi_ready, s)
                    pe.wait_ge(xlo_ready, s)
                for t in range(T):
                    mm = pe.transpose(b_xt[:, t * P:(t + 1) * P], x_sb[s][:, t, :], ident[:, :])
                mm.then_inc(xt_ready, 1)

            def x_part(s):
                pe.wait_ge(xhi_ready, s + 1)
                pe.wait_ge(xlo_ready, s + 1)
                for k, g in enumerate(gate_order):
                    if s >= 1:
                        pe.wait_ge(gate_read, 4 * (s - 1) + k + 1)
                    wc = slice(g * D, (g + 1) * D)
                    pe.matmul(big[k][:, :], w_hi[:, wc], xt_hi[s % 2][:, :], start=True, stop=False)
                    pe.matmul(big[k][:, :], w_lo[:, wc], xt_hi[s % 2][:, :], start=False, stop=False)
                    mm = pe.matmul(big[k][:, :], w_hi[:, wc], xt_lo[s % 2][:, :], start=False, stop=(s == 0))
                    if s == 0:
                        mm.then_inc(gate_ready, 1)

            def h_part(s):
                pe.wait_ge(hhi_ready, s)
                for k, g in enumerate(gate_order):
                    wc = slice(g * D, (g + 1) * D)
                    pe.matmul(big[k][:, :], u_hi[:, wc], h_hi[:, :], start=False, stop=False)
                    pe.matmul(big[k][:, :], u_lo[:, wc], h_hi[:, :], start=False, stop=False)
                    if k == 0:
                        pe.wait_ge(hlo_ready, s)
                    pe.matmul(big[k][:, :], u_hi[:, wc], h_lo[:, :], start=False, stop=True).then_inc(gate_ready, 1)

            def turn_h(s):
                pe.wait_ge(h_ready, s + 1)
                if s >= 1:
                    pe.wait_ge(y_ready, s)
                for t in range(T):
                    mm = pe.transpose(b_ht[:, t * P:(t + 1) * P], h2[:, t * P:(t + 1) * P], ident[:, :])
                mm.then_inc(ht_ready, 1)

            def turn_xn(s):
                pe.wait_ge(xn_ready, T * (s + 1))
                if s >= 1:
                    pe.wait_ge(xnt_copied, s)
                for t in range(T):
                    mm = pe.transpose(b_xnt[:, t * P:(t + 1) * P], rows[:, s * T + t, 0:D], ident[:, :])
                mm.then_inc(xnt_ready, 1)

            def logits(s):
                pe.wait_ge(xnt_copied, s + 1)
                if s % GB == 0 and s > 0:
                    pe.wait_ge(route_step, RS * (s // GB - 1) + 2)
                if s % GB == 1 and s > GB:
                    pe.wait_ge(slot_step, 7 * (s // GB - 1) + 3)
                for t in range(T):
                    mm = pe.matmul(lg_ps[:, (s % GB) * T + t, :], xnt[:, t * P:(t + 1) * P], rw[:, :], start=True, stop=True)
                mm.then_inc(logits_ready, 1)

            def places(b):
                pe.wait_ge(chosen_ready, b + 1)
                for g in range(GB):
                    for c in range(2):
                        lo = g * T
                        pe.matmul(pl_ps[:, c, lo:lo + T, :], before[:, :], chosen[:, c, lo:lo + T, :], start=True, stop=True)
                        for j in range(1, T):
                            pe.matmul(pl_ps[:, c, lo + j:lo + T, :], ones_b[:, :], chosen[:, c, lo:lo + T - j, :],
                                      start=False, stop=True, skip_group_check=True)
                    for t in range(T):
                        mm = pe.matmul(cn_ps[:, g, :], ones_b[:, :], chosen[:, 0, g * T + t, :], start=(t == 0), stop=(t == T - 1))
                mm.then_inc(places_ready, 1)

            pe.wait_ge(pool_consts, 4)
            turn_x(0)
            turn_x(1)
            pe.wait_ge(dve_consts, 3)
            pe.wait_ge(act_consts, 2)
            x_part(0)
            for s in range(S + 3):
                if 1 <= s < S:
                    h_part(s)
                if 0 <= s - 2 < S:
                    logits(s - 2)
                if s >= 4 and s % 2 == 0 or s == S + 2:
                    if (s - 4) // 2 < NB:
                        places((s - 4) // 2)
                if s + 1 < S:
                    x_part(s + 1)
                if s + 2 < S:
                    turn_x(s + 2)
                if 0 <= s - 1 < S:
                    turn_xn(s - 1)
                if s < S:
                    turn_h(s)

            def turn_xd(u):
                pe.wait_ge(xd_in[u % 4], 16 * (u // 4 + 1))
                if u >= 1:
                    pe.wait_ge(xdhi_ready, u)
                    pe.wait_ge(xdlo_ready, u)
                for k in range(HALF):
                    mm = pe.transpose(b_xt[:, k * P:(k + 1) * P], xd[u % 4][:, k, 0:D], ident[:, :])
                mm.then_inc(xdt_ready, 1)

            def first(u, k):
                e, _ = unit(u)
                q, n = e % 2, u * NCH + k
                if n >= 2:
                    pe.wait_ge(hid_ready, n - 1)
                if k == 0:
                    pe.wait_ge(ehi_ready, e + 1)
                    pe.wait_ge(elo_ready, e + 1)
                    pe.wait_ge(xdhi_ready, u + 1)
                    pe.wait_ge(xdlo_ready, u + 1)
                if k < FULL:
                    parts = [(0, k * P, P), (1, W1C + k * P, P)]
                else:
                    parts = [(0, WTC, 64 + TAIL)]
                for half, c0, m in parts:
                    dst = big[2 * (n % 2) + half][0:m, :]
                    pe.matmul(dst, e_hi[q][:, c0:c0 + m], xdt_hi[u % 2][:, :], start=True, stop=False)
                    pe.matmul(dst, e_lo[q][:, c0:c0 + m], xdt_hi[u % 2][:, :], start=False, stop=False)
                    mm = pe.matmul(dst, e_hi[q][:, c0:c0 + m], xdt_lo[u % 2][:, :], start=False, stop=True)
                    mm.then_inc(pre_ready, 1)

            def second(u, k):
                e, _ = unit(u)
                q, n = e % 2, u * NCH + k
                if k == 0 and u >= 2:
                    pe.wait_ge(yt_copied, u - 1)
                kk = P if k < FULL else TAIL
                c0, r = WOC + k * P, n % RH
                pe.wait_ge(hidhi_ready, n + 1)
                pe.matmul(b_y[u % 2][:, :], e_hi[q][0:kk, c0:c0 + P], hid_hi[r][0:kk, :], start=(k == 0), stop=False)
                pe.matmul(b_y[u % 2][:, :], e_lo[q][0:kk, c0:c0 + P], hid_hi[r][0:kk, :], start=False, stop=False)
                pe.wait_ge(hidlo_ready, n + 1)
                mm = pe.matmul(b_y[u % 2][:, :], e_hi[q][0:kk, c0:c0 + P], hid_lo[r][0:kk, :], start=False, stop=(k == FULL))
                mm.then_inc(chunk_used, 1)
                return mm

            def turn_y(u):
                pe.wait_ge(yt_copied, u + 1)
                if u >= 1:
                    pe.wait_ge(contrib_ready, 2 * u)
                for k in range(HALF):
                    mm = pe.transpose(b_rt[:, k * P:(k + 1) * P], yt[:, k * C:(k + 1) * C], ident[:, :])
                mm.then_inc(eo_ready, 1)

            turn_xd(0)
            for u in range(NU):
                for k in range(NCH + 2):
                    if k < NCH:
                        first(u, k)
                    if k == 1 and u >= 1:
                        turn_y(u - 1)
                    if k == 3 and u + 1 < NU:
                        turn_xd(u + 1)
                    if k >= 2:
                        second(u, k - 2)
            turn_y(NU - 1)

        @block.scalar
        def _(act):
            def high_x(s):
                act.wait_ge(xt_ready, s + 1)
                if s >= 2:
                    act.wait_ge(gate_ready, 4 * (s - 1))
                nc.scalar.activation(xt_hi[s % 2][:, :], b_xt[:, :], ACT.Copy).then_inc(xhi_ready, 1)

            act.wait_ge(consts_in, 64)
            nc.scalar.activation(w_hi[:, :], w_raw[:, :], ACT.Copy).then_inc(act_consts, 1)
            high_x(0)
            act.wait_ge(dve_consts, 1)
            nc.scalar.activation(u_hi[:, :], u_half[:, :], ACT.Copy).then_inc(act_consts, 1)
            high_x(1)
            for s in range(S + 3):
                if s < S:
                    if s == 0:
                        act.wait_ge(dve_consts, 2)
                    for k in range(4):
                        act.wait_ge(gate_ready, 4 * s + k + 1)
                        nc.scalar.activation(act_g[k][:, :], big[k][:, :], ACT.Tanh, bias=bias_g[:, gate_order[k]:gate_order[k] + 1],
                                             scale=1.0 if k == 2 else 0.5).then_inc(gate_read, 1)
                    act.wait_ge(cell_ready, s + 1)
                    nc.scalar.activation(tanh_c[:, :], cell2[:, :], ACT.Tanh, scale=0.5).then_inc(tanh_ready, 1)
                    act.wait_ge(h_ready, s + 1)
                    nc.scalar.activation(h_hi[:, :], h2[:, :], ACT.Copy).then_inc(hhi_ready, 1)
                if s + 2 < S:
                    high_x(s + 2)
                if 0 <= s - 1 < S:
                    act.wait_ge(xnt_ready, s)
                    if s >= 2:
                        act.wait_ge(logits_ready, s - 1)
                    nc.scalar.activation(xnt[:, :], b_xnt[:, :], ACT.Copy).then_inc(xnt_copied, 1)
                if s >= 3 and s % 2 == 1:
                    b = (s - 3) // 2
                    act.wait_ge(route_step, RS * b + 2)
                    nc.scalar.activation(ex[:, :, :], lg[:, :, :], ACT.Exp).then_inc(exp_ready, 1)

            def high_xd(u):
                act.wait_ge(xdt_ready, u + 1)
                if u >= 2:
                    act.wait_ge(pre_ready, (2 * FULL + 1) * (u - 1))
                nc.scalar.activation(xdt_hi[u % 2][:, :], b_xt[:, :], ACT.Copy).then_inc(xdhi_ready, 1)

            def high_hid(u, k):
                n = u * NCH + k
                m = P if k < FULL else TAIL
                act.wait_ge(hid_ready, n + 1)
                nc.scalar.activation(hid_hi[n % RH][0:m, :], hid[n % RH][0:m, :], ACT.Copy).then_inc(hidhi_ready, 1)

            high_xd(0)
            for u in range(NU):
                for k in range(NCH):
                    n = u * NCH + k
                    m = P if k < FULL else TAIL
                    if n >= RH:
                        act.wait_ge(chunk_used, n - RH + 1)
                    act.wait_ge(pre_ready, (2 * FULL + 1) * u + 2 * k + 1)
                    nc.scalar.activation(act0[n % RH][0:m, :], big[2 * (n % 2)][0:m, :], ACT.Gelu_apprx_tanh).then_inc(gelu_ready, 1)
                    if k >= 1:
                        high_hid(u, k - 1)
                    if k == 3 and u + 1 < NU:
                        high_xd(u + 1)
                high_hid(u, NCH - 1)
                act.wait_ge(chunk_used, NCH * (u + 1))
                if u >= 1:
                    act.wait_ge(eo_ready, u)
                nc.scalar.activation(yt[:, :], b_y[u % 2][:, :], ACT.Copy).then_inc(yt_copied, 1)



        @block.vector
        def _(dve):
            def low_x(s):
                dve.wait_ge(xhi_ready, s + 1)
                dve.tensor_tensor(xt_lo[s % 2][:, :], b_xt[:, :], xt_hi[s % 2][:, :], ALU.subtract).then_inc(xlo_ready, 1)

            def bc(ap):
                return ap.unsqueeze(2).broadcast_to([P, BT, E])

            dve.wait_ge(consts_in, 64)
            dve.tensor_scalar(u_half[:, :], u_raw[:, :], 0.5, None, ALU.mult).then_inc(dve_consts, 1)
            dve.wait_ge(act_consts, 1)
            dve.tensor_scalar(bias_g[:, 0:3], bias[:, 0:3], 0.5, None, ALU.mult)
            dve.tensor_copy(bias_g[:, 3:4], bias[:, 3:4]).then_inc(dve_consts, 1)
            dve.tensor_tensor(w_lo[:, :], w_raw[:, :], w_hi[:, :], ALU.subtract).then_inc(dve_consts, 1)
            low_x(0)
            dve.wait_ge(act_consts, 2)
            dve.tensor_tensor(u_lo[:, :], u_half[:, :], u_hi[:, :], ALU.subtract).then_inc(dve_consts, 1)
            low_x(1)
            dve.wait_ge(pool_consts, 7)
            dve.tensor_scalar(rows[:, :, D:D + 1], toknum_i[:, :].unsqueeze(2), -FAR, None, ALU.add)
            dve.tensor_copy(slot0[:, :, :], slot0_i[:, :, :])
            dve.tensor_copy(rev[:, :, :], rev_i[:, :, :]).then_inc(dve_consts, 1)

            def inverse_root(v, x, y, p, base):
                dve.tensor_scalar(x, v, EPS, None, ALU.add).then_inc(root_step, 1)
                dve.wait_ge(root_step, base + 1)
                dve.tensor_scalar(y.bitcast(I32), x.bitcast(I32), -0.5, float(0x5f3759df), ALU.mult, ALU.add).then_inc(root_step, 1)
                for n in range(3):
                    dve.wait_ge(root_step, base + 3 * n + 2)
                    dve.tensor_tensor(p, y, y, ALU.mult).then_inc(root_step, 1)
                    dve.wait_ge(root_step, base + 3 * n + 3)
                    dve.scalar_tensor_tensor(out=p, in0=p, scalar=-0.5, in1=x, op0=ALU.mult, op1=ALU.mult).then_inc(root_step, 1)
                    dve.wait_ge(root_step, base + 3 * n + 4)
                    dve.scalar_tensor_tensor(out=y, in0=p, scalar=1.5, in1=y, op0=ALU.add, op1=ALU.mult).then_inc(root_step, 1)
                dve.wait_ge(root_step, base + RT)

            def norm(s):
                dve.wait_ge(ht_ready, s + 1)
                dve.scalar_tensor_tensor(out=y_sb[:, :, :], in0=b_ht[:, :].rearrange("p (t d) -> p t d", t=T), scalar=0.5,
                                         in1=x_sb[s][:, :, :], op0=ALU.mult, op1=ALU.add).then_inc(y_ready, 1)
                dve.wait_ge(y_ready, s + 1)
                for t in range(T):
                    dve.bn_stats(stats[:, t, :], y_sb[:, t, :]).then_inc(stats_ready, 1)
                for t in range(T):
                    dve.wait_ge(stats_ready, T * s + t + 1)
                    dve.bn_aggr(moments[:, t, :], stats[:, t, :]).then_inc(mom_ready, 1)
                dve.wait_ge(mom_ready, T * (s + 1))
                inverse_root(moments[:, :, 1], var_eps[:, :], rstd[:, :], newton[:, :], RT * s)
                for t in range(T):
                    dve.tensor_scalar(rows[:, s * T + t, 0:D], y_sb[:, t, :], moments[:, t, 0:1], rstd[:, t:t + 1],
                                      ALU.subtract, ALU.mult).then_inc(xn_ready, 1)

            def choose(b):
                r = RS * b
                dve.wait_ge(logits_ready, GB * (b + 1))
                dve.tensor_reduce(col[:, :], lg_ps, AX.X, ALU.max).then_inc(route_step, 1)
                dve.wait_ge(route_step, r + 1)
                dve.tensor_tensor(lg[:, :, :], lg_ps, bc(col[:, :]), ALU.subtract).then_inc(route_step, 1)
                dve.wait_ge(exp_ready, b + 1)
                dve.tensor_reduce(col[:, :], ex[:, :, :], AX.X, ALU.add).then_inc(route_step, 1)
                dve.wait_ge(route_step, r + 3)
                dve.reciprocal(rsum[:, :], col[:, :]).then_inc(route_step, 1)
                dve.wait_ge(route_step, r + 4)
                dve.tensor_tensor(raw[:, :, :], ex[:, :, :], bc(rsum[:, :]), ALU.mult).then_inc(route_step, 1)
                n = r + 5
                for c, left in enumerate([raw, rest]):
                    dve.wait_ge(route_step, n)
                    dve.tensor_reduce(gates[:, c, :], left[:, :, :], AX.X, ALU.max).then_inc(route_step, 1)
                    dve.wait_ge(route_step, n + 1)
                    dve.tensor_tensor(eq[:, :, :], left[:, :, :], bc(gates[:, c, :]), ALU.is_equal).then_inc(route_step, 1)
                    dve.wait_ge(route_step, n + 2)
                    dve.tensor_tensor(eq[:, :, :], eq[:, :, :], rev[:, :, :], ALU.mult).then_inc(route_step, 1)
                    dve.wait_ge(route_step, n + 3)
                    dve.tensor_reduce(col[:, :], eq[:, :, :], AX.X, ALU.max).then_inc(route_step, 1)
                    dve.wait_ge(route_step, n + 4)
                    one_hot = dve.tensor_tensor(chosen[:, c, :, :], eq[:, :, :], bc(col[:, :]), ALU.is_equal)
                    if c == 0:
                        one_hot.then_inc(route_step, 1)
                        dve.wait_ge(route_step, n + 5)
                        dve.tensor_tensor(picked[:, :, :], raw[:, :, :], chosen[:, 0, :, :], ALU.mult).then_inc(picked_ready, 1)
                        dve.wait_ge(picked_ready, 3 * b + 1)
                        dve.tensor_tensor(rest[:, :, :], raw[:, :, :], picked[:, :, :], ALU.subtract).then_inc(picked_ready, 1)
                        dve.wait_ge(picked_ready, 3 * b + 2)
                    else:
                        one_hot.then_inc(chosen_ready, 1)
                    n += 5
                dve.wait_ge(chosen_ready, b + 1)
                dve.tensor_tensor(rest[:, :, :], rest[:, :, :], chosen[:, 1, :, :], ALU.mult).then_inc(picked_ready, 1)
                dve.wait_ge(picked_ready, 3 * b + 3)
                dve.tensor_tensor(rows[:, b * BT:(b + 1) * BT, D + 1:ROW], picked[:, :, :], rest[:, :, :], ALU.add).then_inc(gatevec_ready, 1)

            def assign(b):
                k = 7 * b
                dve.wait_ge(places_ready, b + 1)
                dve.tensor_scalar(cnt[:, :, :], cn_ps, float(C), None, ALU.min).then_inc(slot_step, 1)
                dve.tensor_copy(place[:, 0, :, :], pl_ps[:, 0, :, :]).then_inc(slot_step, 1)
                dve.wait_ge(slot_step, k + 2)
                dve.tensor_tensor(place[:, 1, :, :].rearrange("p (g t) e -> p g t e", g=GB),
                                  pl_ps[:, 1, :, :].rearrange("p (g t) e -> p g t e", g=GB),
                                  cnt[:, :, :].unsqueeze(2).broadcast_to([P, GB, T, E]), ALU.add).then_inc(slot_step, 1)
                dve.wait_ge(slot_step, k + 3)
                dve.tensor_scalar(over[:, :, :, :], place[:, :, :, :], float(C), FAR, ALU.is_ge, ALU.mult).then_inc(slot_step, 1)
                dve.wait_ge(slot_step, k + 4)
                dve.tensor_tensor(over[:, :, :, :], over[:, :, :, :], place[:, :, :, :], ALU.add).then_inc(slot_step, 1)
                dve.wait_ge(slot_step, k + 5)
                dve.tensor_tensor(over[:, :, :, :], over[:, :, :, :],
                                  slot0[:, :, :].unsqueeze(1).broadcast_to([P, 2, BT, E]), ALU.add).then_inc(slot_step, 1)
                dve.wait_ge(slot_step, k + 6)
                dve.tensor_tensor(over[:, :, :, :], over[:, :, :, :], chosen[:, :, :, :], ALU.mult).then_inc(slot_step, 1)
                dve.wait_ge(slot_step, k + 7)
                dve.tensor_reduce(slot_f[:, :, :], over[:, :, :, :], AX.X, ALU.add).then_inc(slotf_ready, 1)
                dve.tensor_scalar(void[:, :, :], gates[:, :, :], 0.0, FAR, ALU.is_equal, ALU.mult).then_inc(slotf_ready, 1)
                dve.wait_ge(slotf_ready, 2 * b + 2)
                dve.wait_ge(gatevec_ready, b + 1)
                dve.scalar_tensor_tensor(out=slot_ix[b][:, :].rearrange("p (c t) -> p c t", c=2), in0=slot_f[:, :, :],
                                         scalar=float(b * GB * E * C), in1=void[:, :, :], op0=ALU.add, op1=ALU.add).then_inc(slots_ready, 1)

            for s in range(S + 3):
                if 0 <= s - 1 < S:
                    norm(s - 1)
                if s < S:
                    if s >= 1:
                        dve.wait_ge(gate_read, 4 * s + 1)
                        dve.scalar_tensor_tensor(out=term_f[:, :], in0=act_g[0][:, :], scalar=1.0, in1=cell2[:, :],
                                                 op0=ALU.add, op1=ALU.mult).then_inc(terms_ready, 1)
                    dve.wait_ge(gate_read, 4 * s + 3)
                    dst = term_i if s else cell2
                    ins = dve.scalar_tensor_tensor(out=dst[:, :], in0=act_g[1][:, :], scalar=1.0, in1=act_g[2][:, :],
                                                   op0=ALU.add, op1=ALU.mult)
                    if s:
                        ins.then_inc(terms_ready, 1)
                        dve.wait_ge(terms_ready, 2 * s)
                        ins = dve.scalar_tensor_tensor(out=cell2[:, :], in0=term_f[:, :], scalar=0.5, in1=term_i[:, :],
                                                       op0=ALU.mult, op1=ALU.add)
                    ins.then_inc(cell_ready, 1)
                if s + 2 < S and s > 0:
                    pass
                if s < S:
                    dve.wait_ge(tanh_ready, s + 1)
                    dve.wait_ge(gate_read, 4 * s + 4)
                    dve.scalar_tensor_tensor(out=h2[:, :], in0=act_g[3][:, :], scalar=1.0, in1=tanh_c[:, :],
                                             op0=ALU.add, op1=ALU.mult).then_inc(h_ready, 1)
                    dve.wait_ge(hhi_ready, s + 1)
                    dve.tensor_tensor(h_lo[:, :], h2[:, :], h_hi[:, :], ALU.subtract).then_inc(hlo_ready, 1)
                if s + 2 < S:
                    low_x(s + 2)
                if s >= 3 and s % 2 == 1:
                    choose((s - 3) // 2)
                if s >= 4 and s % 2 == 0:
                    assign((s - 4) // 2)
            def low_xd(u):
                dve.wait_ge(xdhi_ready, u + 1)
                dve.tensor_tensor(xdt_lo[u % 2][:, :], b_xt[:, :], xdt_hi[u % 2][:, :], ALU.subtract).then_inc(xdlo_ready, 1)

            def low_hid(u, k):
                n = u * NCH + k
                m = P if k < FULL else TAIL
                dve.wait_ge(hidhi_ready, n + 1)
                dve.tensor_tensor(hid_lo[n % RH][0:m, :], hid[n % RH][0:m, :], hid_hi[n % RH][0:m, :], ALU.subtract).then_inc(hidlo_ready, 1)

            def give(u):
                e, _ = unit(u)
                dve.wait_ge(eo_ready, u + 1)
                if u >= 2:
                    dve.wait_ge(added[u % 2], 16 * HALF * (u // 2))
                dve.tensor_tensor(contrib[u % 2][:, :, :], b_rt[:, :].rearrange("p (g d) -> p g d", g=HALF),
                                  xd[u % 4][:, :, D + 1 + e:D + 2 + e].broadcast_to([P, HALF, D]), ALU.mult).then_inc(contrib_ready, 1)
                dve.tensor_scalar(token_ix[u % 2][:, :], xd[u % 4][:, :, D], FAR, None, ALU.add).then_inc(contrib_ready, 1)

            low_xd(0)
            for u in range(NU):
                for k in range(NCH):
                    n = u * NCH + k
                    m = P if k < FULL else TAIL
                    dve.wait_ge(gelu_ready, n + 1)
                    dve.wait_ge(pre_ready, (2 * FULL + 1) * u + min(2 * k + 2, 2 * FULL + 1))
                    b1 = big[2 * (n % 2) + 1][:, :] if k < FULL else big[2 * (n % 2)][64:64 + TAIL, :]
                    dve.tensor_tensor(hid[n % RH][0:m, :], act0[n % RH][0:m, :], b1, ALU.mult).then_inc(hid_ready, 1)
                    if k >= 1:
                        low_hid(u, k - 1)
                    if k == 3 and u + 1 < NU:
                        low_xd(u + 1)
                    if k == 2 and u >= 1:
                        give(u - 1)
                low_hid(u, NCH - 1)
            give(NU - 1)

            for g in range(S):
                dve.wait_ge(fin_in[g], 16)
                for t in range(T):
                    dve.bn_stats(fin_stats[:, g, t, :], fin[g][:, t, :]).then_inc(fstats_ready, 1)
                for t in range(T):
                    dve.wait_ge(fstats_ready, T * g + t + 1)
                    dve.bn_aggr(fin_mom[:, g, t, :], fin_stats[:, g, t, :]).then_inc(fmom_ready, 1)
                dve.wait_ge(fmom_ready, T * (g + 1))
                inverse_root(fin_mom[:, g, :, 1], var_eps[:, :], fin_rstd[:, g, :], newton[:, :], RT * (S + g))
                for t in range(T):
                    dve.tensor_scalar(fin[g][:, t, :], fin[g][:, t, :], fin_mom[:, g, t, 0:1], fin_rstd[:, g, t:t + 1],
                                      ALU.subtract, ALU.mult).then_inc(fin_ready, 1)


_INS = ['L0_attn_input_seq', 'L0_attn_w', 'L0_attn_u', 'L0_attn_bias', 'L0_ffn_router_w', 'L0_ffn_w0_kernel',
        'L0_ffn_w1_kernel', 'L0_ffn_wo_kernel']


def kernel(**inputs):
    import numpy as np
    import concourse.bacc as bacc
    from concourse import mybir as mb
    from concourse.bass_utils import run_bass_kernel_spmd as run

    nc = bacc.Bacc("TRN2", target_bir_lowering=False, num_devices=1)
    arrays, args = {}, []
    for name in _INS:
        a = np.ascontiguousarray(inputs[name])
        arrays[f"in_{name}_dram"] = a
        args.append(nc.dram_tensor(f"in_{name}_dram", a.shape, mb.dt.from_np(a.dtype), kind="ExternalInput").ap())
    shape = inputs['L0_attn_input_seq'].shape
    out = nc.dram_tensor("out_0_dram", shape, mb.dt.float32, kind="ExternalOutput").ap()
    build(nc, *args, out)
    r = run(nc, [arrays], core_ids=[0])
    return r.results[0]["out_0_dram"]
```

```python
from contextlib import ExitStack

import concourse.bass as bass
from concourse import mybir

F32 = mybir.dt.float32
F32R = mybir.dt.float32r
BF16 = mybir.dt.bfloat16
U32 = mybir.dt.uint32
I32 = mybir.dt.int32
ALU = mybir.AluOpType
ACT = mybir.ActivationFunctionType
AX = mybir.AxisListType


def build(nc, x_in, w_in, u_in, b_in, rw_in, w0_in, w1_in, wo_in, out):
    S, N, D = x_in.shape
    P = 128
    assert D == P
    E, _, H = w0_in.shape
    T = N // P
    C = (int(2.0 * N / E) + 3) // 4 * 4
    assert C == P
    EPS = 1e-5
    FULL = H // P
    TAIL = H - FULL * P
    HALF = S // 2
    ROW = D + 1 + E
    FAR = float(1 << 20)
    GB = 2
    BT = GB * T
    NB = S // GB
    W1C, WTC, WOC = FULL * P, 2 * FULL * P, (2 * FULL + 1) * P
    WCOLS = WOC + (FULL + 1) * P
    NCH = FULL + 1
    RT = 12
    RING_E = 3
    PIECES = 4
    AS = 6
    RH = 3

    gate_order = [1, 0, 3, 2]

    with ExitStack() as ctx:
        def sb(name, shape, dt=F32):
            return ctx.enter_context(nc.sbuf_tensor(name, shape, dt))

        def bank(name):
            return ctx.enter_context(nc.psum_tensor(name, [P, 512], F32))

        def sem(name):
            return ctx.enter_context(nc.semaphore(name))

        slots = nc.dram_tensor("slots", [S * E * C, ROW], F32, kind="Internal").ap()
        tokens = nc.dram_tensor("tokens", [S * N, D], F32, kind="Internal").ap()

        ident = sb("ident", [P, P])
        ones = sb("ones", [P, P])
        ones_b = sb("ones_b", [P, P], BF16)
        before = sb("before", [P, P], BF16)
        zero_rows = sb("zero_rows", [P, E * ROW])
        w_raw = sb("w_raw", [P, 4 * D])
        u_raw = sb("u_raw", [P, 4 * D])
        w_hi, w_lo = sb("w_hi", [P, 4 * D], F32R), sb("w_lo", [P, 4 * D], F32R)
        u_half = sb("u_half", [P, 4 * D])
        u_hi, u_lo = sb("u_hi", [P, 4 * D], F32R), sb("u_lo", [P, 4 * D], F32R)
        bias = sb("bias", [P, 4])
        bias_g = sb("bias_g", [P, 4])
        rw = sb("rw", [P, E])
        x_sb = [sb(f"x{s}", [P, T, D]) for s in range(S)]
        xt_hi = [sb(f"xt_hi{q}", [P, N], F32R) for q in range(2)]
        xt_lo = [sb(f"xt_lo{q}", [P, N], F32R) for q in range(2)]
        act_g = [sb(f"act_g{k}", [P, N]) for k in range(4)]
        term_f, term_i = sb("term_f", [P, N]), sb("term_i", [P, N])
        cell2 = sb("cell2", [P, N])
        tanh_c = sb("tanh_c", [P, N])
        h2 = sb("h2", [P, N])
        h_hi, h_lo = sb("h_hi", [P, N], F32R), sb("h_lo", [P, N], F32R)
        y_sb = [sb(f"y_sb{q}", [P, T, D]) for q in range(2)]
        stats = sb("stats", [P, T, 6])
        moments = [sb(f"moments{q}", [P, T, 2]) for q in range(2)]
        fin_mom = sb("fin_mom", [P, S * T, 2])
        fin_stats = sb("fin_stats", [P, S * T, 6])
        root_x, root_y = sb("root_x", [P, 2, S * T]), sb("root_y", [P, 2, S * T])
        root_p, root_b = sb("root_p", [P, 2, S * T]), sb("root_b", [P, 2, S * T])
        rows = sb("rows", [P, S * T, ROW])
        xnt = sb("xnt", [P, N])
        toknum_i = sb("toknum_i", [P, S * T], I32)
        expert_i = sb("expert_i", [P, BT, 2, E], I32)
        group0_i = sb("group0_i", [P, BT, 2], I32)
        expert_no = sb("expert_no", [P, BT, 2, E])
        group0 = sb("group0", [P, BT, 2])
        top = sb("top", [P, BT, E])
        top_ix = sb("top_ix", [P, BT, E], U32)
        less, ex = sb("less", [P, BT, E]), sb("ex", [P, BT, E])
        total, rtotal = sb("total", [P, BT]), sb("rtotal", [P, BT])
        gates = sb("gates", [P, BT, 2])
        choice = sb("choice", [P, BT, 2])
        chosen = sb("chosen", [P, BT, 2, E], BF16)
        gate_rows = sb("gate_rows", [P, BT, 2, E])
        base = sb("base", [P, BT, 2])
        void = sb("void", [P, BT, 2])
        cnt = sb("cnt", [P, GB, 2, E])
        place = sb("place", [P, BT, 2, E])
        pos = sb("pos", [P, BT, 2])
        over = sb("over", [P, BT, 2])
        slot_ix = [sb(f"slot_ix{b}", [P, 2 * BT], U32) for b in range(NB)]
        e_raw = [sb(f"e_raw{q}", [P, WCOLS]) for q in range(2)]
        e_hi = [sb(f"e_hi{q}", [P, WCOLS], F32R) for q in range(RING_E)]
        e_lo = [sb(f"e_lo{q}", [P, WCOLS], F32R) for q in range(RING_E)]
        xd = [sb(f"xd{r}", [P, HALF, ROW]) for r in range(4)]
        xdt_hi = [sb(f"xdt_hi{q}", [P, HALF * C], F32R) for q in range(2)]
        xdt_lo = [sb(f"xdt_lo{q}", [P, HALF * C], F32R) for q in range(2)]
        act0 = act_g[0:RH]
        hid = [term_f, term_i, cell2]
        hid_hi = [sb(f"hid_hi{r}", [P, 512], F32R) for r in range(RH)]
        hid_lo = [sb(f"hid_lo{r}", [P, 512], F32R) for r in range(RH)]
        yt = tanh_c
        contrib = [sb(f"contrib{q}", [P, HALF, D]) for q in range(2)]
        token_ix = [sb(f"token_ix{q}", [P, HALF], U32) for q in range(2)]
        fin = x_sb

        big = [bank(f"big{k}") for k in range(4)]
        b_xt, b_ht, b_xnt, b_rt = bank("b_xt"), bank("b_ht"), bank("b_xnt"), bank("b_rt")
        lg_ps = b_rt[:, 0:BT * E].rearrange("p (t e) -> p t e", e=E)
        pl_ps = b_rt[:, 128:128 + 2 * BT * E].rearrange("p (t c e) -> p t c e", c=2, e=E)
        cn_ps = b_rt[:, 256:256 + GB * E].rearrange("p (g e) -> p g e", e=E)
        b_y = [b_ht, b_xnt]

        consts_in = sem("consts_in")
        x_in_s = [sem(f"x_in{s}") for s in range(S)]
        zeros_made, zeros_out = sem("zeros_made"), sem("zeros_out")
        pool_consts, dve_consts, act_consts = sem("pool_consts"), sem("dve_consts"), sem("act_consts")
        xt_ready, xhi_ready, xlo_ready = sem("xt_ready"), sem("xhi_ready"), sem("xlo_ready")
        gate_ready, gate_read = sem("gate_ready"), sem("gate_read")
        terms_ready, cell_ready, tanh_ready = sem("terms_ready"), sem("cell_ready"), sem("tanh_ready")
        h_ready, hhi_ready, hlo_ready, ht_ready = sem("h_ready"), sem("hhi_ready"), sem("hlo_ready"), sem("ht_ready")
        y_ready, stats_ready, mom_ready, root_step = sem("y_ready"), sem("stats_ready"), sem("mom_ready"), sem("root_step")
        xn_ready, xnt_ready, xnt_copied = sem("xn_ready"), sem("xnt_ready"), sem("xnt_copied")
        logits_ready, exp_ready = sem("logits_ready"), sem("exp_ready")
        top_ready, topix_ready, gates_step = sem("top_ready"), sem("topix_ready"), sem("gates_step")
        base_step = sem("base_step")
        chosen_ready, places_ready, slot_step = sem("chosen_ready"), sem("places_ready"), sem("slot_step")
        resid_out = sem("resid_out")
        gate_rows_in = sem("gate_rows_in")
        routed = [sem(f"routed{b}") for b in range(NB)]
        raw_in = [sem(f"raw_in{q}") for q in range(2)]
        raw_clear, ehi_ready, elo_ready = sem("raw_clear"), sem("ehi_ready"), sem("elo_ready")
        xd_in = [sem(f"xd_in{r}") for r in range(4)]
        xdt_ready, xdhi_ready, xdlo_ready = sem("xdt_ready"), sem("xdhi_ready"), sem("xdlo_ready")
        pre_ready, gelu_ready, hid_ready = sem("pre_ready"), sem("gelu_ready"), sem("hid_ready")
        hidhi_ready, hidlo_ready, chunk_used = sem("hidhi_ready"), sem("hidlo_ready"), sem("chunk_used")
        y_done, yt_copied, eo_ready = sem("y_done"), sem("yt_copied"), sem("eo_ready")
        contrib_ready, added = sem("contrib_ready"), [sem(f"added{q}") for q in range(2)]
        fin_in = [sem(f"fin_in{g}") for g in range(S)]
        fstats_ready, fmom_ready = sem("fstats_ready"), sem("fmom_ready")
        fin_ready = [sem(f"fin_ready{g}") for g in range(S)]
        out_done = sem("out_done")

        fin_cols = [slice(0, HALF * T), slice(HALF * T, (HALF + 2) * T), slice((HALF + 2) * T, S * T)]

        def fin_root(g):
            return [c.start <= g * T < c.stop for c in fin_cols].index(True)

        NU = 2 * E

        units = [(e, half) for e0 in range(0, E, RING_E) for half in range(2) for e in range(e0, min(e0 + RING_E, E))]

        def unit(u):
            return units[u]

        def units_until(e, half):
            return units.index((e, half)) + 1

        def piece(n):
            return slice(n * WCOLS // PIECES, (n + 1) * WCOLS // PIECES)

        block = ctx.enter_context(nc.Block())

        @block.sync
        def _(sp):
            def load_x(s):
                sp.dma_start(x_sb[s][:, :, :], x_in[s].rearrange("(t p) i -> p t i", p=P)).then_inc(x_in_s[s], 16)

            def load_expert(e):
                q = e % 2
                if e < 2:
                    sp.wait_ge(raw_clear, 2)
                else:
                    sp.wait_ge(elo_ready, PIECES * (e - 1))
                r = e_raw[q]
                for k, (src, dst) in enumerate([
                        (w0_in[e, :, 0:FULL * P], r[:, 0:W1C]), (w1_in[e, :, 0:FULL * P], r[:, W1C:WTC]),
                        (w0_in[e, :, FULL * P:H], r[:, WTC:WTC + TAIL]),
                        (w1_in[e, :, FULL * P:H], r[:, WTC + 64:WTC + 64 + TAIL]),
                        (wo_in[e, 0:FULL * P, :].rearrange("(k p) m -> p k m", p=P),
                         r[:, WOC:WOC + FULL * P].rearrange("p (k m) -> p k m", k=FULL)),
                        (wo_in[e, FULL * P:H, :], r[0:TAIL, WOC + FULL * P:WCOLS])]):
                    sp.dma_start(dst, src).then_inc(raw_in[q], 16)

            def zero_slots(g):
                n = E * C
                sp.dma_start(slots[g * n:(g + 1) * n, :].rearrange("(p r) f -> p (r f)", p=P), zero_rows[:, :]).then_inc(zeros_out, 16)

            load_x(0)
            sp.dma_start(w_raw[:, :], w_in[:, :]).then_inc(consts_in, 16)
            sp.dma_start(bias[:, :], b_in.rearrange("(g h) -> h g", g=4), allow_slow_non_contiguous=True).then_inc(consts_in, 16)
            sp.dma_start(u_raw[:, :], u_in[:, :]).then_inc(consts_in, 16)
            sp.dma_start(rw[:, :], rw_in[:, :]).then_inc(consts_in, 16)
            for s in range(1, 4):
                load_x(s)
            load_expert(0)
            sp.wait_ge(zeros_made, 1)
            for g in range(GB):
                zero_slots(g)
            for s in range(4, S):
                load_x(s)
            load_expert(1)
            for g in range(GB, S):
                zero_slots(g)
            for s in range(S):
                if s == 2:
                    load_expert(2)
                sp.wait_ge(xn_ready, T * (s + 1))
                sp.dma_start(tokens[s * N:(s + 1) * N, :].rearrange("(t p) d -> p t d", p=P),
                             rows[:, s * T:(s + 1) * T, 0:D]).then_inc(resid_out, 16)

            def load_xd(u):
                e, half = unit(u)
                r = u % 4
                for b in range(NB // 2 * half, NB // 2 * (half + 1)):
                    sp.wait_ge(routed[b], 16 * 2 * BT)
                if u >= 4:
                    sp.wait_ge(xdt_ready, u - 3)
                    sp.wait_ge(contrib_ready, 2 * (u - 3))
                sp.dma_start(xd[r][:, :, :], slots.rearrange("(g e c) f -> e c g f", g=S, e=E)[
                    e, :, HALF * half:HALF * (half + 1), :]).then_inc(xd_in[r], 16)

            load_xd(0)
            load_xd(1)
            next_e = 3
            for u in range(NU):
                if u + 2 < NU:
                    load_xd(u + 2)
                while next_e < E and (next_e < 5 or units_until(next_e - 5, 1) <= u - 1):
                    load_expert(next_e)
                    next_e += 1

            for g in range(S):
                u = NU - 3 if g < HALF else NU - 1
                for q in range(2):
                    last = u if u % 2 == q else u - 1
                    sp.wait_ge(added[q], 16 * HALF * (last // 2 + 1))
                sp.dma_start(fin[g][:, :, :], tokens[g * N:(g + 1) * N, :].rearrange("(t p) d -> p t d", p=P)).then_inc(fin_in[g], 16)
            for g in range(S):
                sp.wait_ge(fin_ready[g], T)
                sp.dma_start(out[g].rearrange("(t p) d -> p t d", p=P), fin[g][:, :, :]).then_inc(out_done, 16)
            sp.wait_ge(out_done, 16 * S)

        @block.gpsimd
        def _(pool):
            pool.memset(zero_rows[:, :], 0.0).then_inc(zeros_made, 1)
            pool.memset(ones[:, :], 1.0).then_inc(pool_consts, 1)
            pool.wait_ge(pool_consts, 1)
            pool.affine_select(ident[:, :], ones[:, :], [[1, P]], ALU.is_equal, 0.0, base=0, channel_multiplier=-1).then_inc(pool_consts, 1)
            pool.memset(ones_b[:, :], 1.0).then_inc(pool_consts, 1)
            pool.wait_ge(pool_consts, 3)
            pool.affine_select(before[:, :], ones_b[:, :], [[1, P]], ALU.is_gt, 0.0, base=0, channel_multiplier=-1).then_inc(pool_consts, 1)
            pool.iota(toknum_i[:, :], [[P, S * T]], base=0, channel_multiplier=1).then_inc(pool_consts, 1)
            pool.iota(expert_i[:, :, :, :], [[0, 2 * BT], [1, E]], base=0, channel_multiplier=0).then_inc(pool_consts, 1)
            pool.iota(group0_i[:, :, :], [[E * C, GB], [0, 2 * T]], base=0, channel_multiplier=0).then_inc(pool_consts, 1)
            for q in range(2):
                pool.memset(e_raw[q][:, WTC:WCOLS], 0.0).then_inc(raw_clear, 1)

            def low_weights(e):
                for n in range(PIECES):
                    pool.wait_ge(ehi_ready, PIECES * e + n + 1)
                    pool.tensor_tensor(e_lo[e % RING_E][:, piece(n)], e_raw[e % 2][:, piece(n)], e_hi[e % RING_E][:, piece(n)],
                                       ALU.subtract).then_inc(elo_ready, 1)

            low_weights(0)
            low_weights(1)
            for b in range(NB):
                if b == 2:
                    low_weights(2)
                if b == 0:
                    pool.wait_ge(zeros_out, 16 * S)
                pool.wait_ge(slot_step, AS * (b + 1))
                pool.wait_ge(gate_rows_in, b + 1)
                for t in range(BT):
                    for c in range(2):
                        pool.indirect_dma_start(
                            slots, bass.IndirectOffsetOnAxis(ap=slot_ix[b][:, 2 * t + c:2 * t + c + 1], axis=0),
                            rows[:, b * BT + t, :], None, bounds_check=S * E * C - 1, oob_is_err=False).then_inc(routed[b], 16)

            pool.wait_ge(resid_out, 16 * S)
            for u in range(NU):
                e, half = unit(u)
                for n in range(RING_E, E):
                    if units_until(n - RING_E, 1) == u:
                        low_weights(n)
                pool.wait_ge(contrib_ready, 2 * (u + 1))
                if u >= 1:
                    pool.wait_ge(added[(u - 1) % 2], 16 * HALF * ((u - 1) // 2 + 1))
                for k in range(HALF):
                    pool.indirect_dma_start(
                        tokens, bass.IndirectOffsetOnAxis(ap=token_ix[u % 2][:, k:k + 1], axis=0),
                        contrib[u % 2][:, k, :], None, bounds_check=S * N - 1, oob_is_err=False,
                        compute_op=ALU.add).then_inc(added[u % 2], 16)

        @block.tensor
        def _(pe):
            def turn_x(s):
                pe.wait_ge(x_in_s[s], 16)
                if s >= 1:
                    pe.wait_ge(xhi_ready, s)
                    pe.wait_ge(xlo_ready, s)
                for t in range(T):
                    mm = pe.transpose(b_xt[:, t * P:(t + 1) * P], x_sb[s][:, t, :], ident[:, :])
                mm.then_inc(xt_ready, 1)

            def x_part(s):
                pe.wait_ge(xhi_ready, s + 1)
                pe.wait_ge(xlo_ready, s + 1)
                for k, g in enumerate(gate_order):
                    if s >= 1:
                        pe.wait_ge(gate_read, 4 * (s - 1) + k + 1)
                    wc = slice(g * D, (g + 1) * D)
                    pe.matmul(big[k][:, :], w_hi[:, wc], xt_hi[s % 2][:, :], start=True, stop=False)
                    pe.matmul(big[k][:, :], w_lo[:, wc], xt_hi[s % 2][:, :], start=False, stop=False)
                    mm = pe.matmul(big[k][:, :], w_hi[:, wc], xt_lo[s % 2][:, :], start=False, stop=(s == 0))
                    if s == 0:
                        mm.then_inc(gate_ready, 1)

            def h_part(s):
                pe.wait_ge(hhi_ready, s)
                for k, g in enumerate(gate_order):
                    wc = slice(g * D, (g + 1) * D)
                    pe.matmul(big[k][:, :], u_hi[:, wc], h_hi[:, :], start=False, stop=False)
                    pe.matmul(big[k][:, :], u_lo[:, wc], h_hi[:, :], start=False, stop=False)
                    if k == 0:
                        pe.wait_ge(hlo_ready, s)
                    pe.matmul(big[k][:, :], u_hi[:, wc], h_lo[:, :], start=False, stop=True).then_inc(gate_ready, 1)

            def turn_h(s):
                pe.wait_ge(h_ready, s + 1)
                if s >= 1:
                    pe.wait_ge(y_ready, s)
                for t in range(T):
                    mm = pe.transpose(b_ht[:, t * P:(t + 1) * P], h2[:, t * P:(t + 1) * P], ident[:, :])
                mm.then_inc(ht_ready, 1)

            def turn_xn(s):
                pe.wait_ge(xn_ready, T * (s + 1))
                if s >= 1:
                    pe.wait_ge(xnt_copied, s)
                for t in range(T):
                    mm = pe.transpose(b_xnt[:, t * P:(t + 1) * P], rows[:, s * T + t, 0:D], ident[:, :])
                mm.then_inc(xnt_ready, 1)

            def logits(s):
                pe.wait_ge(xnt_copied, s + 1)
                if s >= GB and s % GB == 0:
                    pe.wait_ge(slot_step, AS * (s // GB - 1) + 2)
                for t in range(T):
                    mm = pe.matmul(lg_ps[:, (s % GB) * T + t, :], xnt[:, t * P:(t + 1) * P], rw[:, :], start=True, stop=True)
                mm.then_inc(logits_ready, 1)

            def places(b):
                pe.wait_ge(chosen_ready, b + 1)
                for g in range(GB):
                    lo = g * T
                    pe.matmul(pl_ps[:, lo:lo + T, :, :], before[:, :], chosen[:, lo:lo + T, :, :], start=True, stop=True)
                    for j in range(1, T):
                        pe.matmul(pl_ps[:, lo + j:lo + T, :, :], ones_b[:, :], chosen[:, lo:lo + T - j, :, :],
                                  start=False, stop=True, skip_group_check=True)
                    for t in range(T):
                        mm = pe.matmul(cn_ps[:, g, :], ones_b[:, :], chosen[:, lo + t, 0, :], start=(t == 0), stop=(t == T - 1))
                mm.then_inc(places_ready, 1)

            pe.wait_ge(pool_consts, 4)
            turn_x(0)
            turn_x(1)
            pe.wait_ge(dve_consts, 3)
            pe.wait_ge(act_consts, 2)
            x_part(0)
            for s in range(S + 3):
                if 1 <= s < S:
                    h_part(s)
                if 0 <= s - 2 < S:
                    turn_xn(s - 2)
                if s >= 4 and s % 2 == 0:
                    places(s // 2 - 2)
                if s + 1 < S:
                    x_part(s + 1)
                if 0 <= s - 2 < S:
                    logits(s - 2)
                if s + 2 < S:
                    turn_x(s + 2)
                if s < S:
                    turn_h(s)

            def turn_xd(u):
                pe.wait_ge(xd_in[u % 4], 16 * (u // 4 + 1))
                if u >= 1:
                    pe.wait_ge(xdhi_ready, u)
                    pe.wait_ge(xdlo_ready, u)
                for k in range(HALF):
                    mm = pe.transpose(b_xt[:, k * P:(k + 1) * P], xd[u % 4][:, k, 0:D], ident[:, :])
                mm.then_inc(xdt_ready, 1)

            def first(u, k):
                e, _ = unit(u)
                q, n = e % RING_E, u * NCH + k
                if n >= 2:
                    pe.wait_ge(hid_ready, n - 1)
                if k == 0:
                    pe.wait_ge(ehi_ready, PIECES * (e + 1))
                    pe.wait_ge(elo_ready, PIECES * (e + 1))
                    pe.wait_ge(xdhi_ready, u + 1)
                    pe.wait_ge(xdlo_ready, u + 1)
                if k < FULL:
                    parts = [(0, k * P, P), (1, W1C + k * P, P)]
                else:
                    parts = [(0, WTC, 64 + TAIL)]
                for half, c0, m in parts:
                    dst = big[2 * (n % 2) + half][0:m, :]
                    pe.matmul(dst, e_hi[q][:, c0:c0 + m], xdt_hi[u % 2][:, :], start=True, stop=False)
                    pe.matmul(dst, e_lo[q][:, c0:c0 + m], xdt_hi[u % 2][:, :], start=False, stop=False)
                    mm = pe.matmul(dst, e_hi[q][:, c0:c0 + m], xdt_lo[u % 2][:, :], start=False, stop=True)
                    mm.then_inc(pre_ready, 1)

            def second(u, k):
                e, _ = unit(u)
                q, n = e % RING_E, u * NCH + k
                if k == 0 and u >= 2:
                    pe.wait_ge(yt_copied, u - 1)
                kk = P if k < FULL else TAIL
                c0, r = WOC + k * P, n % RH
                pe.wait_ge(hidhi_ready, n + 1)
                pe.matmul(b_y[u % 2][:, :], e_hi[q][0:kk, c0:c0 + P], hid_hi[r][0:kk, :], start=(k == 0), stop=False)
                pe.matmul(b_y[u % 2][:, :], e_lo[q][0:kk, c0:c0 + P], hid_hi[r][0:kk, :], start=False, stop=False)
                pe.wait_ge(hidlo_ready, n + 1)
                mm = pe.matmul(b_y[u % 2][:, :], e_hi[q][0:kk, c0:c0 + P], hid_lo[r][0:kk, :], start=False, stop=(k == FULL))
                mm.then_inc(chunk_used, 1)
                return mm

            def turn_y(u):
                pe.wait_ge(yt_copied, u + 1)
                if u >= 1:
                    pe.wait_ge(contrib_ready, 2 * u)
                for k in range(HALF):
                    mm = pe.transpose(b_rt[:, k * P:(k + 1) * P], yt[:, k * C:(k + 1) * C], ident[:, :])
                mm.then_inc(eo_ready, 1)

            turn_xd(0)
            for u in range(NU):
                for k in range(NCH + 2):
                    if k < NCH:
                        first(u, k)
                    if k == 1 and u >= 1:
                        turn_y(u - 1)
                    if k == 3 and u + 1 < NU:
                        turn_xd(u + 1)
                    if k >= 2:
                        second(u, k - 2)
            turn_y(NU - 1)

        @block.scalar
        def _(act):
            def high_x(s):
                act.wait_ge(xt_ready, s + 1)
                if s >= 2:
                    act.wait_ge(gate_ready, 4 * (s - 1))
                nc.scalar.activation(xt_hi[s % 2][:, :], b_xt[:, :], ACT.Copy).then_inc(xhi_ready, 1)

            act.wait_ge(consts_in, 64)
            nc.scalar.activation(w_hi[:, :], w_raw[:, :], ACT.Copy).then_inc(act_consts, 1)
            high_x(0)
            act.wait_ge(dve_consts, 1)
            nc.scalar.activation(u_hi[:, :], u_half[:, :], ACT.Copy).then_inc(act_consts, 1)
            high_x(1)
            def high_weights(e, n):
                if n == 0:
                    act.wait_ge(raw_in[e % 2], 96 * (e // 2 + 1))
                    if e >= RING_E:
                        act.wait_ge(chunk_used, NCH * units_until(e - RING_E, 1))
                nc.scalar.activation(e_hi[e % RING_E][:, piece(n)], e_raw[e % 2][:, piece(n)], ACT.Copy).then_inc(ehi_ready, 1)

            for s in range(S + 3):
                if s >= 4 and s % 2 == 0:
                    b = s // 2 - 2
                    act.wait_ge(top_ready, (BT + 1) * (b + 1))
                    nc.scalar.activation(ex[:, :, :], less[:, :, :], ACT.Exp).then_inc(exp_ready, 1)
                if s < S:
                    if s == 0:
                        act.wait_ge(dve_consts, 2)
                    for k in range(4):
                        act.wait_ge(gate_ready, 4 * s + k + 1)
                        nc.scalar.activation(act_g[k][:, :], big[k][:, :], ACT.Tanh, bias=bias_g[:, gate_order[k]:gate_order[k] + 1],
                                             scale=1.0 if k == 2 else 0.5).then_inc(gate_read, 1)
                if 0 <= s - 2 < S:
                    act.wait_ge(xnt_ready, s - 1)
                    if s >= 3:
                        act.wait_ge(logits_ready, s - 2)
                    nc.scalar.activation(xnt[:, :], b_xnt[:, :], ACT.Copy).then_inc(xnt_copied, 1)
                if s < S:
                    act.wait_ge(cell_ready, s + 1)
                    nc.scalar.activation(tanh_c[:, :], cell2[:, :], ACT.Tanh, scale=0.5).then_inc(tanh_ready, 1)
                    act.wait_ge(h_ready, s + 1)
                    nc.scalar.activation(h_hi[:, :], h2[:, :], ACT.Copy).then_inc(hhi_ready, 1)
                if s + 2 < S:
                    high_x(s + 2)
                if 0 <= s - 1 < S:
                    act.wait_ge(root_step, RT * s)
                    q = (s - 1) % 2
                    for t in range(T):
                        nc.scalar.activation(rows[:, (s - 1) * T + t, 0:D], y_sb[q][:, t, :], ACT.Identity,
                                             bias=root_b[:, q, t:t + 1], scale=root_y[:, q, t:t + 1]).then_inc(xn_ready, 1)
                if 1 <= s < 1 + RING_E * PIECES // 2:
                    for n in range(2 * (s - 1), 2 * s):
                        high_weights(n // PIECES, n % PIECES)

            def high_xd(u):
                act.wait_ge(xdt_ready, u + 1)
                if u >= 2:
                    act.wait_ge(pre_ready, (2 * FULL + 1) * (u - 1))
                nc.scalar.activation(xdt_hi[u % 2][:, :], b_xt[:, :], ACT.Copy).then_inc(xdhi_ready, 1)

            def high_hid(u, k):
                n = u * NCH + k
                m = P if k < FULL else TAIL
                act.wait_ge(hid_ready, n + 1)
                nc.scalar.activation(hid_hi[n % RH][0:m, :], hid[n % RH][0:m, :], ACT.Copy).then_inc(hidhi_ready, 1)

            high_xd(0)
            for u in range(NU):
                for k in range(NCH):
                    n = u * NCH + k
                    m = P if k < FULL else TAIL
                    if n >= RH:
                        act.wait_ge(chunk_used, n - RH + 1)
                    act.wait_ge(pre_ready, (2 * FULL + 1) * u + 2 * k + 1)
                    nc.scalar.activation(act0[n % RH][0:m, :], big[2 * (n % 2)][0:m, :], ACT.Gelu_apprx_tanh).then_inc(gelu_ready, 1)
                    if k >= 1:
                        high_hid(u, k - 1)
                    if k == 3 and u + 1 < NU:
                        high_xd(u + 1)
                    for e in range(RING_E, E):
                        if units_until(e - RING_E, 1) == u and k < PIECES:
                            high_weights(e, k)
                high_hid(u, NCH - 1)
                act.wait_ge(chunk_used, NCH * (u + 1))
                if u >= 1:
                    act.wait_ge(eo_ready, u)
                nc.scalar.activation(yt[:, :], b_y[u % 2][:, :], ACT.Copy).then_inc(yt_copied, 1)

            for g in range(0, S, 2):
                act.wait_ge(root_step, RT * (S + fin_root(g) + 1))
                for t in range(T):
                    n = g * T + t
                    nc.scalar.activation(fin[g][:, t, :], fin[g][:, t, :], ACT.Identity,
                                         bias=root_b[:, 1, n:n + 1], scale=root_y[:, 1, n:n + 1]).then_inc(fin_ready[g], 1)



        @block.vector
        def _(dve):
            def low_x(s):
                dve.wait_ge(xhi_ready, s + 1)
                dve.tensor_tensor(xt_lo[s % 2][:, :], b_xt[:, :], xt_hi[s % 2][:, :], ALU.subtract).then_inc(xlo_ready, 1)

            dve.wait_ge(consts_in, 64)
            dve.tensor_scalar(u_half[:, :], u_raw[:, :], 0.5, None, ALU.mult).then_inc(dve_consts, 1)
            dve.wait_ge(act_consts, 1)
            dve.tensor_scalar(bias_g[:, 0:3], bias[:, 0:3], 0.5, None, ALU.mult)
            dve.tensor_copy(bias_g[:, 3:4], bias[:, 3:4]).then_inc(dve_consts, 1)
            dve.tensor_tensor(w_lo[:, :], w_raw[:, :], w_hi[:, :], ALU.subtract).then_inc(dve_consts, 1)
            low_x(0)
            dve.wait_ge(act_consts, 2)
            dve.tensor_tensor(u_lo[:, :], u_half[:, :], u_hi[:, :], ALU.subtract).then_inc(dve_consts, 1)
            low_x(1)
            dve.wait_ge(pool_consts, 7)
            dve.tensor_scalar(rows[:, :, D:D + 1], toknum_i[:, :].unsqueeze(2), -FAR, None, ALU.add)
            dve.tensor_copy(expert_no[:, :, :, :], expert_i[:, :, :, :])
            dve.tensor_copy(group0[:, :, :], group0_i[:, :, :])
            dve.memset(cnt[:, :, :, :], 0.0).then_inc(dve_consts, 1)
            dve.wait_ge(dve_consts, 5)

            def root(i, n):
                if i < S:
                    a, m = (slice(None), i % 2, slice(0, T)), moments[i % 2]
                else:
                    a, m = (slice(None), 1, fin_cols[i - S]), fin_mom[:, fin_cols[i - S], :]
                x, y, p, b = root_x[a], root_y[a], root_p[a], root_b[a]
                if n:
                    dve.wait_ge(root_step, RT * i + n)
                if n == 0:
                    ins = dve.tensor_scalar(x, m[:, :, 1], EPS, None, ALU.add)
                elif n == 1:
                    ins = dve.tensor_scalar(y.bitcast(I32), x.bitcast(I32), -0.5, float(0x5f3759df), ALU.mult, ALU.add)
                elif n == RT - 1:
                    ins = dve.scalar_tensor_tensor(out=b, in0=m[:, :, 0], scalar=-1.0, in1=y, op0=ALU.mult, op1=ALU.mult)
                elif n % 3 == 2:
                    ins = dve.tensor_tensor(p, y, y, ALU.mult)
                elif n % 3 == 0:
                    ins = dve.scalar_tensor_tensor(out=p, in0=p, scalar=-0.5, in1=x, op0=ALU.mult, op1=ALU.mult)
                else:
                    ins = dve.scalar_tensor_tensor(out=y, in0=p, scalar=1.5, in1=y, op0=ALU.add, op1=ALU.mult)
                ins.then_inc(root_step, 1)

            def roots(s, first, last):
                if 0 <= s - 1 < S:
                    for n in range(first, last):
                        root(s - 1, n)

            def sum_h(s):
                if 0 <= s < S:
                    dve.wait_ge(ht_ready, s + 1)
                    if s >= 2:
                        dve.wait_ge(xn_ready, T * (s - 1))
                    dve.scalar_tensor_tensor(out=y_sb[s % 2][:, :, :], in0=b_ht[:, :].rearrange("p (t d) -> p t d", t=T), scalar=0.5,
                                             in1=x_sb[s][:, :, :], op0=ALU.mult, op1=ALU.add).then_inc(y_ready, 1)

            def stat(s, t):
                if 0 <= s < S:
                    dve.wait_ge(y_ready, s + 1)
                    dve.bn_stats(stats[:, t, :], y_sb[s % 2][:, t, :]).then_inc(stats_ready, 1)

            def moment(s):
                if 0 <= s < S:
                    for t in range(T):
                        dve.wait_ge(stats_ready, T * s + t + 1)
                        ins = dve.bn_aggr(moments[s % 2][:, t, :], stats[:, t, :])
                    ins.then_inc(mom_ready, 1)
                    dve.wait_ge(mom_ready, s + 1)

            def choose(b, s):
                k = 5 * b
                dve.wait_ge(logits_ready, GB * (b + 1))
                for t in range(BT):
                    dve.max(top[:, t, :], lg_ps[:, t, :]).then_inc(top_ready, 1)
                dve.wait_ge(top_ready, (BT + 1) * b + BT)
                dve.tensor_tensor(less[:, :, :], top[:, :, :], top[:, :, 0:1].broadcast_to([P, BT, E]), ALU.subtract).then_inc(top_ready, 1)
                for t in range(BT):
                    ins = dve.max_index(top_ix[:, t, :], top[:, t, :], lg_ps[:, t, :])
                ins.then_inc(topix_ready, 1)
                sum_h(s)
                dve.wait_ge(exp_ready, b + 1)
                dve.tensor_reduce(total[:, :], ex[:, :, :], AX.X, ALU.add).then_inc(gates_step, 1)
                stat(s, 0)
                dve.wait_ge(gates_step, k + 1)
                dve.reciprocal(rtotal[:, :], total[:, :]).then_inc(gates_step, 1)
                stat(s, 1)
                dve.wait_ge(gates_step, k + 2)
                dve.tensor_tensor(gates[:, :, :], ex[:, :, 0:2], rtotal[:, :].unsqueeze(2).broadcast_to([P, BT, 2]), ALU.mult).then_inc(gates_step, 1)
                stat(s, 2)
                dve.wait_ge(gates_step, k + 3)
                dve.wait_ge(topix_ready, b + 1)
                dve.scalar_tensor_tensor(out=choice[:, :, :], in0=gates[:, :, :], scalar=0.0, in1=top_ix[:, :, 0:2],
                                         op0=ALU.is_gt, op1=ALU.mult).then_inc(gates_step, 1)
                stat(s, 3)
                dve.wait_ge(gates_step, k + 4)
                dve.tensor_tensor(chosen[:, :, :, :], expert_no[:, :, :, :], choice[:, :, :].unsqueeze(3).broadcast_to([P, BT, 2, E]),
                                  ALU.is_equal).then_inc(chosen_ready, 1)
                dve.scalar_tensor_tensor(out=base[:, :, :], in0=choice[:, :, :], scalar=float(C), in1=group0[:, :, :],
                                         op0=ALU.mult, op1=ALU.add).then_inc(base_step, 1)
                dve.tensor_scalar(void[:, :, :], gates[:, :, :], 0.0, FAR, ALU.is_equal, ALU.mult).then_inc(base_step, 1)
                moment(s)
                dve.wait_ge(base_step, 3 * b + 2)
                dve.scalar_tensor_tensor(out=base[:, :, :], in0=base[:, :, :], scalar=float(b * GB * E * C), in1=void[:, :, :],
                                         op0=ALU.add, op1=ALU.add).then_inc(base_step, 1)
                dve.wait_ge(chosen_ready, b + 1)
                dve.tensor_tensor(gate_rows[:, :, :, :], chosen[:, :, :, :], gates[:, :, :].unsqueeze(3).broadcast_to([P, BT, 2, E]),
                                  ALU.mult).then_inc(gates_step, 1)

            def assign(s, n):
                b = s // 2 - 2
                if s < 4 or s % 2:
                    return
                if n == 0:
                    dve.wait_ge(places_ready, b + 1)
                    ins = dve.tensor_scalar(cnt[:, :, 1, :], cn_ps, float(C), None, ALU.min)
                else:
                    dve.wait_ge(slot_step, AS * b + n)
                if n == 1:
                    for g in range(GB):
                        ins = dve.tensor_tensor(place[:, g * T:(g + 1) * T, :, :], pl_ps[:, g * T:(g + 1) * T, :, :],
                                                cnt[:, g:g + 1, :, :].broadcast_to([P, T, 2, E]), ALU.add)
                elif n == 2:
                    ins = dve.tensor_tensor(place[:, :, :, :], place[:, :, :, :], chosen[:, :, :, :], ALU.mult)
                elif n == 3:
                    ins = dve.tensor_reduce(pos[:, :, :], place[:, :, :, :], AX.X, ALU.add)
                elif n == 4:
                    dve.wait_ge(base_step, 3 * (b + 1))
                    dve.tensor_scalar(over[:, :, :], pos[:, :, :], float(C), FAR, ALU.is_ge, ALU.mult)
                    ins = dve.tensor_tensor(pos[:, :, :], pos[:, :, :], base[:, :, :], ALU.add)
                elif n == 5:
                    ins = dve.tensor_tensor(slot_ix[b][:, :].rearrange("p (t c) -> p t c", c=2), pos[:, :, :], over[:, :, :], ALU.add)
                ins.then_inc(slot_step, 1)

            def gate_row(s):
                b = s // 2 - 2
                if s >= 4 and s % 2 == 0:
                    dve.wait_ge(gates_step, 5 * (b + 1))
                    dve.tensor_tensor(rows[:, b * BT:(b + 1) * BT, D + 1:ROW], gate_rows[:, :, 0, :], gate_rows[:, :, 1, :], ALU.add).then_inc(gate_rows_in, 1)

            for s in range(S + 3):
                if s >= 4 and s % 2 == 0:
                    choose(s // 2 - 2, s - 1)
                else:
                    sum_h(s - 1)
                    for t in range(T):
                        stat(s - 1, t)
                    moment(s - 1)
                if 1 <= s < S:
                    dve.wait_ge(gate_read, 4 * s + 1)
                    dve.scalar_tensor_tensor(out=term_f[:, :], in0=act_g[0][:, :], scalar=1.0, in1=cell2[:, :],
                                             op0=ALU.add, op1=ALU.mult).then_inc(terms_ready, 1)
                roots(s, 0, 1)
                assign(s, 0)
                if s < S:
                    dve.wait_ge(gate_read, 4 * s + 3)
                    ins = dve.scalar_tensor_tensor(out=term_i[:, :] if s else cell2[:, :], in0=act_g[1][:, :], scalar=1.0,
                                                   in1=act_g[2][:, :], op0=ALU.add, op1=ALU.mult)
                    ins.then_inc(terms_ready if s else cell_ready, 1)
                roots(s, 1, 2)
                assign(s, 1)
                if 1 <= s < S:
                    dve.wait_ge(terms_ready, 2 * s)
                    dve.scalar_tensor_tensor(out=cell2[:, :], in0=term_f[:, :], scalar=0.5, in1=term_i[:, :],
                                             op0=ALU.mult, op1=ALU.add).then_inc(cell_ready, 1)
                roots(s, 2, 3)
                assign(s, 2)
                roots(s, 3, 4)
                assign(s, 3)
                roots(s, 4, 5)
                if s < S:
                    dve.wait_ge(tanh_ready, s + 1)
                    dve.wait_ge(gate_read, 4 * s + 4)
                    dve.scalar_tensor_tensor(out=h2[:, :], in0=act_g[3][:, :], scalar=1.0, in1=tanh_c[:, :],
                                             op0=ALU.add, op1=ALU.mult).then_inc(h_ready, 1)
                roots(s, 5, 6)
                assign(s, 4)
                roots(s, 6, 7)
                if s < S:
                    dve.wait_ge(hhi_ready, s + 1)
                    dve.tensor_tensor(h_lo[:, :], h2[:, :], h_hi[:, :], ALU.subtract).then_inc(hlo_ready, 1)
                assign(s, 5)
                roots(s, 7, 8)
                gate_row(s)
                roots(s, 8, 9)
                if s + 2 < S:
                    low_x(s + 2)
                roots(s, 9, RT)

            def low_xd(u):
                dve.wait_ge(xdhi_ready, u + 1)
                dve.tensor_tensor(xdt_lo[u % 2][:, :], b_xt[:, :], xdt_hi[u % 2][:, :], ALU.subtract).then_inc(xdlo_ready, 1)

            def low_hid(u, k):
                n = u * NCH + k
                m = P if k < FULL else TAIL
                dve.wait_ge(hidhi_ready, n + 1)
                dve.tensor_tensor(hid_lo[n % RH][0:m, :], hid[n % RH][0:m, :], hid_hi[n % RH][0:m, :], ALU.subtract).then_inc(hidlo_ready, 1)

            def give(u):
                e, _ = unit(u)
                dve.wait_ge(eo_ready, u + 1)
                if u >= 2:
                    dve.wait_ge(added[u % 2], 16 * HALF * (u // 2))
                dve.tensor_tensor(contrib[u % 2][:, :, :], b_rt[:, :].rearrange("p (g d) -> p g d", g=HALF),
                                  xd[u % 4][:, :, D + 1 + e:D + 2 + e].broadcast_to([P, HALF, D]), ALU.mult).then_inc(contrib_ready, 1)
                dve.tensor_scalar(token_ix[u % 2][:, :], xd[u % 4][:, :, D], FAR, None, ALU.add).then_inc(contrib_ready, 1)

            low_xd(0)
            for u in range(NU):
                for k in range(NCH):
                    n = u * NCH + k
                    m = P if k < FULL else TAIL
                    dve.wait_ge(gelu_ready, n + 1)
                    dve.wait_ge(pre_ready, (2 * FULL + 1) * u + min(2 * k + 2, 2 * FULL + 1))
                    b1 = big[2 * (n % 2) + 1][:, :] if k < FULL else big[2 * (n % 2)][64:64 + TAIL, :]
                    dve.tensor_tensor(hid[n % RH][0:m, :], act0[n % RH][0:m, :], b1, ALU.mult).then_inc(hid_ready, 1)
                    if k >= 1:
                        low_hid(u, k - 1)
                    if k == 3 and u + 1 < NU:
                        low_xd(u + 1)
                    if k == 2 and u >= 1:
                        give(u - 1)
                low_hid(u, NCH - 1)
            give(NU - 1)

            def fin_stat(n):
                g, t = divmod(n, T)
                dve.wait_ge(fin_in[g], 16)
                dve.bn_stats(fin_stats[:, n, :], fin[g][:, t, :]).then_inc(fstats_ready, 1)

            def fin_moment(n):
                dve.wait_ge(fstats_ready, n + 1)
                dve.bn_aggr(fin_mom[:, n, :], fin_stats[:, n, :]).then_inc(fmom_ready, 1)

            def fin_rows(g):
                dve.wait_ge(root_step, RT * (S + fin_root(g) + 1))
                for t in range(T):
                    n = g * T + t
                    dve.tensor_scalar(fin[g][:, t, :], fin[g][:, t, :], fin_mom[:, n, 0:1], root_y[:, 1, n:n + 1],
                                      ALU.subtract, ALU.mult).then_inc(fin_ready[g], 1)

            done = 0
            for i, cols in enumerate(fin_cols):
                for n in range(done, cols.stop):
                    fin_stat(n)
                for n in range(done, cols.stop):
                    fin_moment(n)
                done = cols.stop
                dve.wait_ge(fmom_ready, done)
                for n in range(RT):
                    root(S + i, n)
                for g in range(1, S, 2):
                    if fin_root(g) == i:
                        fin_rows(g)


_INS = ['L0_attn_input_seq', 'L0_attn_w', 'L0_attn_u', 'L0_attn_bias', 'L0_ffn_router_w', 'L0_ffn_w0_kernel',
        'L0_ffn_w1_kernel', 'L0_ffn_wo_kernel']


def kernel(**inputs):
    import numpy as np
    import concourse.bacc as bacc
    from concourse import mybir as mb
    from concourse.bass_utils import run_bass_kernel_spmd as run

    nc = bacc.Bacc("TRN2", target_bir_lowering=False, num_devices=1)
    arrays, args = {}, []
    for name in _INS:
        a = np.ascontiguousarray(inputs[name])
        arrays[f"in_{name}_dram"] = a
        args.append(nc.dram_tensor(f"in_{name}_dram", a.shape, mb.dt.from_np(a.dtype), kind="ExternalInput").ap())
    shape = inputs['L0_attn_input_seq'].shape
    out = nc.dram_tensor("out_0_dram", shape, mb.dt.float32, kind="ExternalOutput").ap()
    build(nc, *args, out)
    r = run(nc, [arrays], core_ids=[0])
    return r.results[0]["out_0_dram"]
```

```python
from contextlib import ExitStack

import concourse.bass as bass
from concourse import mybir

F32 = mybir.dt.float32
F32R = mybir.dt.float32r
BF16 = mybir.dt.bfloat16
U32 = mybir.dt.uint32
I32 = mybir.dt.int32
ALU = mybir.AluOpType
ACT = mybir.ActivationFunctionType
AX = mybir.AxisListType


def build(nc, x_in, w_in, u_in, b_in, rw_in, w0_in, w1_in, wo_in, out):
    S, N, D = x_in.shape
    P = 128
    assert D == P
    E, _, H = w0_in.shape
    T = N // P
    C = (int(2.0 * N / E) + 3) // 4 * 4
    assert C == P
    EPS = 1e-5
    FULL = H // P
    TAIL = H - FULL * P
    HALF = S // 2
    ROW = D + 1 + E
    FAR = float(1 << 20)
    GB = 2
    BT = GB * T
    NB = S // GB
    W1C, WTC, WOC = FULL * P, 2 * FULL * P, (2 * FULL + 1) * P
    WCOLS = WOC + (FULL + 1) * P
    NCH = FULL + 1
    RT = 12
    RING_E = 3
    LOADS = 7
    PIECES = 4
    AS = 6
    RH = 4

    gate_order = [1, 0, 3, 2]

    with ExitStack() as ctx:
        def sb(name, shape, dt=F32):
            return ctx.enter_context(nc.sbuf_tensor(name, shape, dt))

        def bank(name):
            return ctx.enter_context(nc.psum_tensor(name, [P, 512], F32))

        def sem(name):
            return ctx.enter_context(nc.semaphore(name))

        slots = nc.dram_tensor("slots", [S * E * C, ROW], F32, kind="Internal").ap()
        tokens = nc.dram_tensor("tokens", [S * N, D], F32, kind="Internal").ap()

        ident = sb("ident", [P, P])
        ones = sb("ones", [P, P])
        ones_b = sb("ones_b", [P, P], BF16)
        before = sb("before", [P, P], BF16)
        zero_rows = sb("zero_rows", [P, E * ROW])
        w_raw = sb("w_raw", [P, 4 * D])
        u_raw = sb("u_raw", [P, 4 * D])
        w_hi, w_lo = sb("w_hi", [P, 4 * D], F32R), sb("w_lo", [P, 4 * D], F32R)
        u_half = sb("u_half", [P, 4 * D])
        bias = sb("bias", [P, 4])
        bias_g = sb("bias_g", [P, 4])
        rw = sb("rw", [P, E])
        x_sb = [sb(f"x{s}", [P, T, D]) for s in range(S)]
        xt_hi = [sb(f"xt_hi{q}", [P, N], F32R) for q in range(2)]
        xt_lo = [sb(f"xt_lo{q}", [P, N], F32R) for q in range(2)]
        act_g = [sb(f"act_g{k}", [P, N]) for k in range(4)]
        term_f, term_i = sb("term_f", [P, N]), sb("term_i", [P, N])
        cell2 = sb("cell2", [P, N])
        tanh_c = sb("tanh_c", [P, N])
        h2 = sb("h2", [P, N])
        y_sb = [sb(f"y_sb{q}", [P, T, D]) for q in range(2)]
        stats = sb("stats", [P, T, 6])
        moments = [sb(f"moments{q}", [P, T, 2]) for q in range(2)]
        fin_mom = sb("fin_mom", [P, S * T, 2])
        fin_stats = sb("fin_stats", [P, S * T, 6])
        root_x, root_y = sb("root_x", [P, 2, S * T]), sb("root_y", [P, 2, S * T])
        eps = sb("eps", [P, 1])
        root_p, root_b = sb("root_p", [P, 2, S * T]), sb("root_b", [P, 2, S * T])
        rows = sb("rows", [P, S * T, ROW])
        xnt = sb("xnt", [P, N])
        toknum_i = sb("toknum_i", [P, S * T], I32)
        expert_i = sb("expert_i", [P, BT, 2, E], I32)
        group0_i = sb("group0_i", [P, BT, 2], I32)
        expert_no = sb("expert_no", [P, BT, 2, E])
        group0 = sb("group0", [P, BT, 2])
        top = sb("top", [P, BT, E])
        top_ix = sb("top_ix", [P, BT, E], U32)
        less, ex = sb("less", [P, BT, E]), sb("ex", [P, BT, E])
        total, rtotal = sb("total", [P, BT]), sb("rtotal", [P, BT])
        gates = sb("gates", [P, BT, 2])
        choice = sb("choice", [P, BT, 2])
        chosen = sb("chosen", [P, BT, 2, E], BF16)
        gate_rows = sb("gate_rows", [P, BT, 2, E])
        base = sb("base", [P, BT, 2])
        void = sb("void", [P, BT, 2])
        cnt = sb("cnt", [P, GB, 2, E])
        place = sb("place", [P, BT, 2, E])
        pos = sb("pos", [P, BT, 2])
        over = sb("over", [P, BT, 2])
        slot_ix = [sb(f"slot_ix{b}", [P, 2 * BT], U32) for b in range(NB)]
        e_raw = [sb(f"e_raw{q}", [P, WCOLS]) for q in range(2)]
        e_hi = [sb(f"e_hi{q}", [P, WCOLS], F32R) for q in range(RING_E)]
        e_lo = [sb(f"e_lo{q}", [P, WCOLS], F32R) for q in range(RING_E)]
        xd = [sb(f"xd{r}", [P, HALF, ROW]) for r in range(4)]
        xdt_hi = [sb(f"xdt_hi{q}", [P, HALF * C], F32R) for q in range(2)]
        xdt_lo = [sb(f"xdt_lo{q}", [P, HALF * C], F32R) for q in range(2)]
        act0 = act_g
        hid = [term_f, term_i, cell2, h2]
        hid_hi = [sb(f"hid_hi{r}", [P, N], F32R) for r in range(RH)]
        hid_lo = [sb(f"hid_lo{r}", [P, N], F32R) for r in range(RH)]
        yt = tanh_c
        contrib = [sb(f"contrib{q}", [P, HALF, D])[:, :, :] for q in range(2)]
        contrib += [zero_rows[:, q * HALF * D:(q + 1) * HALF * D].rearrange("p (g d) -> p g d", g=HALF) for q in range(2)]
        CR = len(contrib)
        token_ix = [sb(f"token_ix{q}", [P, HALF], U32) for q in range(CR)]
        fin = x_sb

        big = [bank(f"big{k}") for k in range(4)]
        b_xt, b_ht, b_xnt, b_rt = bank("b_xt"), bank("b_ht"), bank("b_xnt"), bank("b_rt")
        lg_ps = b_rt[:, 0:BT * E].rearrange("p (t e) -> p t e", e=E)
        pl_ps = b_rt[:, 128:128 + 2 * BT * E].rearrange("p (t c e) -> p t c e", c=2, e=E)
        cn_ps = b_rt[:, 256:256 + GB * E].rearrange("p (g e) -> p g e", e=E)
        b_y = [b_ht, b_xnt]

        w_loaded, bias_loaded, u_loaded, rw_loaded = sem("w_loaded"), sem("bias_loaded"), sem("u_loaded"), sem("rw_loaded")
        x_in_s = [sem(f"x_in{s}") for s in range(S)]
        zeros_made, zeros_out = sem("zeros_made"), sem("zeros_out")
        pool_consts, dve_consts, act_consts = sem("pool_consts"), sem("dve_consts"), sem("act_consts")
        xt_ready, xhi_ready, xlo_ready = sem("xt_ready"), sem("xhi_ready"), sem("xlo_ready")
        gate_ready, gate_read = sem("gate_ready"), sem("gate_read")
        terms_ready, cell_ready, tanh_ready = sem("terms_ready"), sem("cell_ready"), sem("tanh_ready")
        h_ready, ht_ready = sem("h_ready"), sem("ht_ready")
        y_ready, stats_ready, mom_ready, root_step = sem("y_ready"), sem("stats_ready"), sem("mom_ready"), sem("root_step")
        xn_ready, xnt_ready, xnt_copied = sem("xn_ready"), sem("xnt_ready"), sem("xnt_copied")
        logits_ready, exp_ready = sem("logits_ready"), sem("exp_ready")
        top_ready, topix_ready, gates_step = sem("top_ready"), sem("topix_ready"), sem("gates_step")
        base_step = sem("base_step")
        chosen_ready, places_ready, slot_step = sem("chosen_ready"), sem("places_ready"), sem("slot_step")
        resid_out = sem("resid_out")
        gate_rows_in = sem("gate_rows_in")
        routed = [sem(f"routed{b}") for b in range(NB)]
        raw_in = [sem(f"raw_in{q}") for q in range(2)]
        raw_clear, elo_ready = sem("raw_clear"), sem("elo_ready")
        ehi_ready = [sem(f"ehi_ready{q}") for q in range(RING_E)]
        xd_in = [sem(f"xd_in{r}") for r in range(4)]
        xdt_ready, xdhi_ready, xdlo_ready = sem("xdt_ready"), sem("xdhi_ready"), sem("xdlo_ready")
        pre_ready, gelu_ready, hid_ready = sem("pre_ready"), sem("gelu_ready"), sem("hid_ready")
        hidhi_ready, hidlo_ready, chunk_used = sem("hidhi_ready"), sem("hidlo_ready"), sem("chunk_used")
        yt_copied, eo_ready = sem("yt_copied"), sem("eo_ready")
        contrib_ready, added = sem("contrib_ready"), [sem(f"added{g}") for g in range(S)]
        fin_in = [sem(f"fin_in{g}") for g in range(S)]
        fstats_ready, fmom_ready, fx_ready = sem("fstats_ready"), sem("fmom_ready"), sem("fx_ready")
        fsqrt_ready, froot_step = sem("fsqrt_ready"), sem("froot_step")
        fin_ready = [sem(f"fin_ready{g}") for g in range(S)]
        out_done = sem("out_done")

        FR = 1 + HALF // GB
        FT = 5
        fin_cols = [slice(0, HALF * T)] + [slice(g * T, (g + GB) * T) for g in range(HALF, S, GB)]

        def fin_root(g):
            return 0 if g < HALF else (g - HALF) // GB + 1

        fin_who = ["aavp"] * HALF + ["aavp", "avvp", "avvp", "avav"]

        quarters = [(g, GB) for g in range(0, S, GB)]
        halves = [(0, HALF), (HALF, HALF)]
        units = [(e, q) for q in quarters for e in range(RING_E)]
        for team in (range(RING_E, RING_E + 2), range(RING_E + 2, E)):
            units += [(e, h) for h in halves for e in team]
        units[-1:] = [(E - 1, q) for q in quarters[NB // 2:]]
        NU = len(units)

        early = [(NU - 3, k) for k in range(2, NCH) for _ in range(2)] + [(NU - 2, k) for k in range(1, 5)]

        def gate_no(s, k):
            return 4 * s + k

        def expert(u):
            return units[u][0]

        def groups(u):
            g0, n = units[u][1]
            return range(g0, g0 + n)

        def width(u):
            return len(groups(u)) * C

        def until(e):
            return max(u for u in range(NU) if expert(u) == e) + 1

        def small(u):
            return len(groups(u)) <= GB

        def pre_banks(n):
            return [n % 4] if small(n // NCH) else [2 * (n % 2), 2 * (n % 2) + 1]

        def pre(n, m):
            w = width(n // NCH)
            b = [big[i] for i in pre_banks(n)]
            if n % NCH == FULL:
                return b[0][0:P // 2, 0:w], b[0][P // 2:P, 0:w]
            return b[0][0:m, 0:w], (b[0][0:m, w:2 * w] if small(n // NCH) else b[1][0:m, 0:w])

        def before_in_banks(n):
            return max([m + 1 for m in range(n) if set(pre_banks(m)) & set(pre_banks(n))], default=0)

        def y_rows(u):
            return b_xt[:, GB * C:GB * C + width(u)] if small(u) else b_rt[:, 0:width(u)]

        def adds(g, u):
            return sum(g in groups(v) for v in range(u))

        def piece(n):
            return slice(n * WCOLS // PIECES, (n + 1) * WCOLS // PIECES)

        def fin_row_by_mean(engine, g, t):
            n = g * T + t
            engine.wait_ge(froot_step, FT * fin_root(g) + 4)
            engine.tensor_scalar(fin[g][:, t, :], fin[g][:, t, :], fin_mom[:, n, 0:1], root_y[:, 1, n:n + 1],
                                 ALU.subtract, ALU.mult).then_inc(fin_ready[g], 1)

        block = ctx.enter_context(nc.Block())

        @block.sync
        def _(sp):
            def load_x(s):
                sp.dma_start(x_sb[s][:, :, :], x_in[s].rearrange("(t p) i -> p t i", p=P)).then_inc(x_in_s[s], 16)

            def load_expert(e):
                q = e % 2
                if e < 2:
                    sp.wait_ge(raw_clear, 2)
                else:
                    sp.wait_ge(elo_ready, PIECES * (e - 1))
                r = e_raw[q]
                for k, (src, dst) in enumerate([
                        (w0_in[e, :, 0:FULL * P], r[:, 0:W1C]), (w1_in[e, :, 0:FULL * P], r[:, W1C:WTC]),
                        (w0_in[e, :, FULL * P:H], r[:, WTC:WTC + TAIL]),
                        (w1_in[e, :, FULL * P:H], r[:, WTC + P // 2:WTC + P // 2 + TAIL]),
                        (wo_in[e, 0:FULL * P, :].rearrange("(k p) m -> p k m", p=P),
                         r[:, WOC:WOC + FULL * P].rearrange("p (k m) -> p k m", k=FULL)),
                        (wo_in[e, FULL * P:H, :], r[0:TAIL, WOC + FULL * P:WCOLS]),
                        (wo_in[e, FULL * P:H, :], r[P // 2:P // 2 + TAIL, WOC + FULL * P:WCOLS])]):
                    sp.dma_start(dst, src).then_inc(raw_in[q], 16)

            def zero_slots(g):
                n = E * C
                sp.dma_start(slots[g * n:(g + 1) * n, :].rearrange("(p r) f -> p (r f)", p=P), zero_rows[:, :]).then_inc(zeros_out, 16)

            load_x(0)
            sp.dma_start(w_raw[:, :], w_in[:, :]).then_inc(w_loaded, 16)
            sp.dma_start(bias[:, :], b_in.rearrange("(g h) -> h g", g=4), allow_slow_non_contiguous=True).then_inc(bias_loaded, 16)
            load_x(1)
            sp.dma_start(u_raw[:, :], u_in[:, :]).then_inc(u_loaded, 16)
            sp.dma_start(rw[:, :], rw_in[:, :]).then_inc(rw_loaded, 16)
            load_expert(0)
            load_x(2)
            load_expert(1)
            load_x(3)
            sp.wait_ge(zeros_made, 1)
            for g in range(S):
                zero_slots(g)
                if g < HALF:
                    load_x(HALF + g)
            load_expert(2)
            def store_residual(s):
                sp.wait_ge(xn_ready, T * (s + 1))
                sp.dma_start(tokens[s * N:(s + 1) * N, :].rearrange("(t p) d -> p t d", p=P),
                             rows[:, s * T:(s + 1) * T, 0:D]).then_inc(resid_out, 16)

            def load_xd(u):
                r, gs = u % 4, groups(u)
                for b in sorted({g // GB for g in gs}):
                    sp.wait_ge(routed[b], 16 * 2 * BT)
                if u >= 4:
                    sp.wait_ge(xdt_ready, u - 3)
                    sp.wait_ge(contrib_ready, 2 * (u - 3))
                sp.dma_start(xd[r][:, 0:len(gs), :], slots.rearrange("(g e c) f -> e c g f", g=S, e=E)[
                    expert(u), :, gs.start:gs.stop, :]).then_inc(xd_in[r], 16)

            for s in range(S - GB):
                store_residual(s)
            for u in range(3):
                load_xd(u)
            for s in range(S - GB, S):
                store_residual(s)
            next_e = 3
            for u in range(NU):
                if 3 <= u + 2 < NU:
                    load_xd(u + 2)
                while next_e < E and (next_e < 5 or until(next_e - 5) <= u - 1):
                    load_expert(next_e)
                    next_e += 1

            for g in range(S):
                sp.wait_ge(added[g], 16 * E)
                sp.dma_start(fin[g][:, :, :], tokens[g * N:(g + 1) * N, :].rearrange("(t p) d -> p t d", p=P)).then_inc(fin_in[g], 16)
            for g in range(S):
                sp.wait_ge(fin_ready[g], T)
                sp.dma_start(out[g].rearrange("(t p) d -> p t d", p=P), fin[g][:, :, :]).then_inc(out_done, 16)
            sp.wait_ge(out_done, 16 * S)

        @block.gpsimd
        def _(pool):
            pool.memset(ones[:, :], 1.0).then_inc(pool_consts, 1)
            pool.wait_ge(pool_consts, 1)
            pool.affine_select(ident[:, :], ones[:, :], [[1, P]], ALU.is_equal, 0.0, base=0, channel_multiplier=-1).then_inc(pool_consts, 1)
            pool.memset(ones_b[:, :], 1.0).then_inc(pool_consts, 1)
            pool.wait_ge(pool_consts, 3)
            pool.affine_select(before[:, :], ones_b[:, :], [[1, P]], ALU.is_gt, 0.0, base=0, channel_multiplier=-1).then_inc(pool_consts, 1)
            pool.iota(toknum_i[:, :], [[P, S * T]], base=0, channel_multiplier=1).then_inc(pool_consts, 1)
            pool.iota(expert_i[:, :, :, :], [[0, 2 * BT], [1, E]], base=0, channel_multiplier=0).then_inc(pool_consts, 1)
            pool.iota(group0_i[:, :, :], [[E * C, GB], [0, 2 * T]], base=0, channel_multiplier=0).then_inc(pool_consts, 1)
            pool.memset(zero_rows[:, :], 0.0).then_inc(zeros_made, 1)
            for q in range(2):
                pool.memset(e_raw[q][:, WTC:WCOLS], 0.0).then_inc(raw_clear, 1)

            def low_weights(e):
                for n in range(PIECES):
                    pool.wait_ge(ehi_ready[e % RING_E], PIECES * (e // RING_E) + n + 1)
                    pool.tensor_tensor(e_lo[e % RING_E][:, piece(n)], e_raw[e % 2][:, piece(n)], e_hi[e % RING_E][:, piece(n)],
                                       ALU.subtract).then_inc(elo_ready, 1)

            for e in range(RING_E):
                low_weights(e)
            def scatter(b, tiles):
                pool.wait_ge(slot_step, AS * (b + 1))
                pool.wait_ge(gate_rows_in, b + 1)
                for t in tiles:
                    for c in range(2):
                        pool.indirect_dma_start(
                            slots, bass.IndirectOffsetOnAxis(ap=slot_ix[b][:, 2 * t + c:2 * t + c + 1], axis=0),
                            rows[:, b * BT + t, :], None, bounds_check=S * E * C - 1, oob_is_err=False).then_inc(routed[b], 16)

            def add(u):
                pool.wait_ge(contrib_ready, 2 * (u + 1))
                for k, g in enumerate(groups(u)):
                    if adds(g, u):
                        pool.wait_ge(added[g], 16 * adds(g, u))
                    pool.indirect_dma_start(
                        tokens, bass.IndirectOffsetOnAxis(ap=token_ix[u % CR][:, k:k + 1], axis=0),
                        contrib[u % CR][:, k, :], None, bounds_check=S * N - 1, oob_is_err=False,
                        compute_op=ALU.add).then_inc(added[g], 16)

            pool.wait_ge(zeros_out, 16 * S)
            for b in range(3):
                scatter(b, range(BT))
            pool.wait_ge(resid_out, 16 * S)
            for u in range(3):
                add(u)
            scatter(3, range(BT))
            for u in range(3, NU):
                for e in range(RING_E, E):
                    if until(e - RING_E) == u + 1:
                        low_weights(e)
                add(u)

            for g in range(S):
                for t in range(T):
                    if fin_who[g][t] == "p":
                        fin_row_by_mean(pool, g, t)

        @block.tensor
        def _(pe):
            def turn_x(s):
                pe.wait_ge(x_in_s[s], 16)
                if s >= 1:
                    pe.wait_ge(xhi_ready, s)
                    pe.wait_ge(xlo_ready, s)
                for t in range(T):
                    mm = pe.transpose(b_xt[:, t * P:(t + 1) * P], x_sb[s][:, t, :], ident[:, :])
                mm.then_inc(xt_ready, 1)

            def x_part_0():
                pe.wait_ge(xhi_ready, 1)
                pe.wait_ge(act_consts, 1)
                for k in range(1, 4):
                    wc = slice(gate_order[k] * D, (gate_order[k] + 1) * D)
                    pe.matmul(big[k][:, :], w_hi[:, wc], xt_hi[0][:, :], start=True, stop=False)
                for k in range(1, 4):
                    wc = slice(gate_order[k] * D, (gate_order[k] + 1) * D)
                    if k == 1:
                        pe.wait_ge(xlo_ready, 1)
                    pe.matmul(big[k][:, :], w_hi[:, wc], xt_lo[0][:, :], start=False, stop=False)
                    if k == 1:
                        pe.wait_ge(dve_consts, 2)
                    pe.matmul(big[k][:, :], w_lo[:, wc], xt_hi[0][:, :], start=False, stop=True).then_inc(gate_ready, 1)

            def x_part(s):
                pe.wait_ge(xhi_ready, s + 1)
                pe.wait_ge(xlo_ready, s + 1)
                for k, g in enumerate(gate_order):
                    if gate_no(s - 1, k):
                        pe.wait_ge(gate_read, gate_no(s - 1, k))
                    wc = slice(g * D, (g + 1) * D)
                    pe.matmul(big[k][:, :], w_hi[:, wc], xt_hi[s % 2][:, :], start=True, stop=False)
                    pe.matmul(big[k][:, :], w_lo[:, wc], xt_hi[s % 2][:, :], start=False, stop=False)
                    pe.matmul(big[k][:, :], w_hi[:, wc], xt_lo[s % 2][:, :], start=False, stop=False)

            def h_part(s):
                pe.wait_ge(h_ready, s)
                if s == 1:
                    pe.wait_ge(dve_consts, 3)
                for k, g in enumerate(gate_order):
                    pe.matmul(big[k][:, :], u_half[:, g * D:(g + 1) * D], h2[:, :], start=False, stop=True).then_inc(gate_ready, 1)

            def turn_h(s):
                pe.wait_ge(h_ready, s + 1)
                if s >= 1:
                    pe.wait_ge(y_ready, s)
                for t in range(T):
                    mm = pe.transpose(b_ht[:, t * P:(t + 1) * P], h2[:, t * P:(t + 1) * P], ident[:, :])
                mm.then_inc(ht_ready, 1)

            def turn_xn(s):
                pe.wait_ge(xn_ready, T * (s + 1))
                if s >= 1:
                    pe.wait_ge(xnt_copied, s)
                for t in range(T):
                    mm = pe.transpose(b_xnt[:, t * P:(t + 1) * P], rows[:, s * T + t, 0:D], ident[:, :])
                mm.then_inc(xnt_ready, 1)

            def logits(s):
                pe.wait_ge(xnt_copied, s + 1)
                if s == 0:
                    pe.wait_ge(rw_loaded, 16)
                if s >= GB and s % GB == 0:
                    pe.wait_ge(slot_step, AS * (s // GB - 1) + 2)
                for t in range(T):
                    mm = pe.matmul(lg_ps[:, (s % GB) * T + t, :], xnt[:, t * P:(t + 1) * P], rw[:, :], start=True, stop=True)
                mm.then_inc(logits_ready, 1)

            def places(b):
                pe.wait_ge(chosen_ready, b + 1)
                for g in range(GB):
                    lo = g * T
                    pe.matmul(pl_ps[:, lo:lo + T, :, :], before[:, :], chosen[:, lo:lo + T, :, :], start=True, stop=True)
                    for j in range(1, T):
                        pe.matmul(pl_ps[:, lo + j:lo + T, :, :], ones_b[:, :], chosen[:, lo:lo + T - j, :, :],
                                  start=False, stop=True, skip_group_check=True)
                    for t in range(T):
                        mm = pe.matmul(cn_ps[:, g, :], ones_b[:, :], chosen[:, lo + t, 0, :], start=(t == 0), stop=(t == T - 1))
                mm.then_inc(places_ready, 1)

            def turn_xd(u):
                pe.wait_ge(xd_in[u % 4], 16 * (u // 4 + 1))
                pe.wait_ge(xlo_ready, S)
                if u >= 1:
                    pe.wait_ge(xdhi_ready, u)
                    pe.wait_ge(xdlo_ready, u)
                if u >= 3 and small(u - 3):
                    pe.wait_ge(contrib_ready, 2 * (u - 2))
                for k in range(len(groups(u))):
                    mm = pe.transpose(b_xt[:, k * P:(k + 1) * P], xd[u % 4][:, k, 0:D], ident[:, :])
                mm.then_inc(xdt_ready, 1)

            pe.wait_ge(pool_consts, 4)
            turn_x(0)
            x_part_0()
            turn_x(1)
            for s in range(S):
                if s >= 1:
                    h_part(s)
                if s >= 2:
                    turn_xn(s - 2)
                if s >= 4 and s % 2 == 0:
                    places(s // 2 - 2)
                if s + 2 < S:
                    turn_x(s + 2)
                if s + 1 < S:
                    x_part(s + 1)
                if s >= 2:
                    logits(s - 2)
                if s == S - 1:
                    turn_xd(0)
                turn_h(s)

            def first(u, k):
                e = expert(u)
                q, n, w = e % RING_E, u * NCH + k, width(u)
                if before_in_banks(n):
                    pe.wait_ge(hid_ready, before_in_banks(n))
                else:
                    pe.wait_ge(gate_read, gate_no(S - 1, 3))
                if k == 0:
                    pe.wait_ge(ehi_ready[e % RING_E], PIECES * (e // RING_E + 1))
                    pe.wait_ge(elo_ready, PIECES * (e + 1))
                    pe.wait_ge(xdhi_ready, u + 1)
                    pe.wait_ge(xdlo_ready, u + 1)
                if k < FULL:
                    parts = list(zip(pre(n, P), (k * P, W1C + k * P), (P, P)))
                else:
                    parts = [(big[pre_banks(n)[0]][:, 0:w], WTC, P)]
                for dst, c0, m in parts:
                    pe.matmul(dst, e_hi[q][:, c0:c0 + m], xdt_hi[u % 2][:, 0:w], start=True, stop=False)
                    pe.matmul(dst, e_lo[q][:, c0:c0 + m], xdt_hi[u % 2][:, 0:w], start=False, stop=False)
                    mm = pe.matmul(dst, e_hi[q][:, c0:c0 + m], xdt_lo[u % 2][:, 0:w], start=False, stop=True)
                    mm.then_inc(pre_ready, 1)

            def second(u, k):
                q, n, w = expert(u) % RING_E, u * NCH + k, width(u)
                if k == 0 and u >= 2:
                    pe.wait_ge(yt_copied, u - 1)
                elif k == 0 and u == 0:
                    pe.wait_ge(y_ready, S)
                elif k == 0:
                    pe.wait_ge(xnt_copied, S)
                c0, r = WOC + k * P, n % RH
                y, hi, lo = b_y[u % 2][:, 0:w], e_hi[q][:, c0:c0 + P], e_lo[q][:, c0:c0 + P]
                pe.wait_ge(hidhi_ready, n + 1)
                if k < FULL:
                    pe.matmul(y, hi, hid_hi[r][:, 0:w], start=(k == 0), stop=False)
                    pe.matmul(y, lo, hid_hi[r][:, 0:w], start=False, stop=False)
                    pe.wait_ge(hidlo_ready, n + 1)
                    mm = pe.matmul(y, hi, hid_lo[r][:, 0:w], start=False, stop=False)
                else:
                    h = P // 2
                    pe.matmul(y, lo[0:h, :], hid_hi[r][0:h, 0:w], start=False, stop=False)
                    pe.wait_ge(hidlo_ready, n + 1)
                    mm = pe.matmul(y, hi, hid_hi[r][:, 0:w], start=False, stop=True)
                mm.then_inc(chunk_used, 1)
                return mm

            def turn_y(u):
                pe.wait_ge(yt_copied, u + 1)
                if u >= 1:
                    pe.wait_ge(contrib_ready, 2 * u)
                if small(u):
                    pe.wait_ge(xdlo_ready, min(u + 3, NU))
                else:
                    pe.wait_ge(slot_step, AS * (NB - 1) + 2)
                for k in range(len(groups(u))):
                    mm = pe.transpose(y_rows(u)[:, k * P:(k + 1) * P], yt[:, k * C:(k + 1) * C], ident[:, :])
                mm.then_inc(eo_ready, 1)

            done = 0
            for u in range(NU):
                for k in range(NCH):
                    if (u, k) == (0, 3):
                        places(NB - 2)
                    elif (u, k) == (0, 5):
                        turn_xn(S - 2)
                    elif (u, k) == (1, 1):
                        logits(S - 2)
                    elif (u, k) == (1, 3):
                        turn_xn(S - 1)
                    elif (u, k) == (1, 5):
                        logits(S - 1)
                    elif (u, k) == (2, 5):
                        places(NB - 1)
                    first(u, k)
                    if k == 3 and u + 1 < NU:
                        turn_xd(u + 1)
                    if k == (NCH - 1 if small(u) else NCH - 2) and u >= 1:
                        turn_y(u - 1)
                    while done <= u * NCH + k - (3 if small(u) else 2):
                        second(*divmod(done, NCH))
                        done += 1
            while done < NU * NCH:
                second(*divmod(done, NCH))
                done += 1
            turn_y(NU - 1)

        @block.scalar
        def _(act):
            def high_x(s):
                act.wait_ge(xt_ready, s + 1)
                if s >= 2:
                    act.wait_ge(gate_ready, gate_no(s - 2, 3))
                nc.scalar.activation(xt_hi[s % 2][:, :], b_xt[:, :], ACT.Copy).then_inc(xhi_ready, 1)

            act.wait_ge(w_loaded, 16)
            nc.scalar.activation(w_hi[:, :], w_raw[:, :], ACT.Copy).then_inc(act_consts, 1)
            high_x(0)

            def high_weights(e, n):
                if n == 0:
                    act.wait_ge(raw_in[e % 2], 16 * LOADS * (e // 2 + 1))
                    if e >= RING_E:
                        act.wait_ge(chunk_used, NCH * until(e - RING_E))
                nc.scalar.activation(e_hi[e % RING_E][:, piece(n)], e_raw[e % 2][:, piece(n)], ACT.Copy).then_inc(ehi_ready[e % RING_E], 1)

            def exp(b):
                act.wait_ge(top_ready, (BT + 1) * (b + 1))
                nc.scalar.activation(ex[:, :, :], less[:, :, :], ACT.Exp).then_inc(exp_ready, 1)

            def copy_xnt(s):
                act.wait_ge(xnt_ready, s + 1)
                if s >= 1:
                    act.wait_ge(logits_ready, s)
                nc.scalar.activation(xnt[:, :], b_xnt[:, :], ACT.Copy).then_inc(xnt_copied, 1)

            def norm_rows(s, tiles=range(T)):
                act.wait_ge(root_step, RT * (s + 1))
                q = s % 2
                for t in tiles:
                    nc.scalar.activation(rows[:, s * T + t, 0:D], y_sb[q][:, t, :], ACT.Identity,
                                         bias=root_b[:, q, t:t + 1], scale=root_y[:, q, t:t + 1]).then_inc(xn_ready, 1)

            for s in range(S):
                if s >= 4 and s % 2 == 0:
                    exp(s // 2 - 2)
                if s == 0:
                    act.wait_ge(dve_consts, 1)
                for k in range(0 if s else 1, 4):
                    act.wait_ge(gate_ready, gate_no(s, k))
                    nc.scalar.activation(act_g[k][:, :], big[k][:, :], ACT.Tanh, bias=bias_g[:, gate_order[k]:gate_order[k] + 1],
                                         scale=1.0 if k == 2 else 0.5).then_inc(gate_read, 1)
                if s >= 2:
                    copy_xnt(s - 2)
                if s == 0:
                    high_x(1)
                elif s <= RING_E + 1:
                    for i in (2 * s - 2, 2 * s - 1):
                        high_weights(1 + i // PIECES, i % PIECES)
                act.wait_ge(cell_ready, s + 1)
                nc.scalar.activation(tanh_c[:, :], cell2[:, :], ACT.Tanh, scale=0.5).then_inc(tanh_ready, 1)
                if s + 2 < S:
                    high_x(s + 2)
                if s == 0:
                    for n in range(PIECES):
                        high_weights(0, n)
                if 1 <= s < S - 1:
                    norm_rows(s - 1)

            def high_xd(u):
                act.wait_ge(xdt_ready, u + 1)
                if u >= 2:
                    act.wait_ge(pre_ready, (2 * FULL + 1) * (u - 1))
                nc.scalar.activation(xdt_hi[u % 2][:, 0:width(u)], b_xt[:, 0:width(u)], ACT.Copy).then_inc(xdhi_ready, 1)

            def high_hid(u, k):
                n = u * NCH + k
                m = P if k < FULL else P // 2
                act.wait_ge(hid_ready, n + 1)
                nc.scalar.activation(hid_hi[n % RH][0:m, 0:width(u)], hid[n % RH][0:m, 0:width(u)], ACT.Copy).then_inc(hidhi_ready, 1)

            def copy_y(u):
                act.wait_ge(chunk_used, NCH * (u + 1))
                if u >= 1:
                    act.wait_ge(eo_ready, u)
                nc.scalar.activation(yt[:, 0:width(u)], b_y[u % 2][:, 0:width(u)], ACT.Copy).then_inc(yt_copied, 1)

            high_xd(0)
            exp(NB - 2)
            for u in range(NU):
                for k in range(NCH):
                    if (u, k) in ((0, 2), (0, 3)):
                        norm_rows(S - 2, range((k - 2) * T // 2, (k - 1) * T // 2))
                    elif (u, k) == (0, 5):
                        copy_xnt(S - 2)
                    elif u == 1 and k < 2:
                        norm_rows(S - 1, range(k * T // 2, (k + 1) * T // 2))
                    elif (u, k) == (1, 3):
                        copy_xnt(S - 1)
                    elif (u, k) == (2, 1):
                        exp(NB - 1)
                    n = u * NCH + k
                    m = P if k < FULL else P // 2
                    if n >= RH:
                        act.wait_ge(chunk_used, n - RH + 1)
                    w = width(u)
                    act.wait_ge(pre_ready, (2 * FULL + 1) * u + 2 * k + (2 if small(u) and k < FULL else 1))
                    nc.scalar.activation(act0[n % RH][0:m, 0:w], pre(n, P)[0], ACT.Gelu_apprx_tanh).then_inc(gelu_ready, 1)
                    if k >= 1:
                        high_hid(u, k - 1)
                    elif u >= 1:
                        high_hid(u - 1, NCH - 1)
                    if k == (3 if small(u) else 2) and u >= 1:
                        copy_y(u - 1)
                    if k == 3 and u + 1 < NU:
                        high_xd(u + 1)
                    for e in range(RING_E, E):
                        if until(e - RING_E) == u and k >= NCH - PIECES:
                            high_weights(e, k - (NCH - PIECES))
            high_hid(NU - 1, NCH - 1)
            copy_y(NU - 1)

            def fin_sqrt(i):
                c = fin_cols[i]
                act.wait_ge(fmom_ready, c.stop)
                nc.scalar.activation(root_p[:, 0, c], fin_mom[:, c, 1], ACT.Sqrt, bias=eps[:, :]).then_inc(fsqrt_ready, 1)

            def fin_rows(g):
                for t in range(T):
                    n = g * T + t
                    if fin_who[g][t] == "a":
                        act.wait_ge(froot_step, FT * (fin_root(g) + 1))
                        nc.scalar.activation(fin[g][:, t, :], fin[g][:, t, :], ACT.Identity,
                                             bias=root_b[:, 1, n:n + 1], scale=root_y[:, 1, n:n + 1]).then_inc(fin_ready[g], 1)

            fin_sqrt(0)
            for g in range(HALF):
                fin_rows(g)
            for i in range(1, FR):
                fin_sqrt(i)
                for g in range(HALF + GB * (i - 1), HALF + GB * i):
                    fin_rows(g)

        @block.vector
        def _(dve):
            def low_x(s):
                dve.wait_ge(xhi_ready, s + 1)
                dve.tensor_tensor(xt_lo[s % 2][:, :], b_xt[:, :], xt_hi[s % 2][:, :], ALU.subtract).then_inc(xlo_ready, 1)

            dve.wait_ge(bias_loaded, 16)
            dve.tensor_scalar(bias_g[:, 0:3], bias[:, 0:3], 0.5, None, ALU.mult)
            dve.tensor_copy(bias_g[:, 3:4], bias[:, 3:4]).then_inc(dve_consts, 1)
            low_x(0)
            dve.wait_ge(act_consts, 1)
            dve.tensor_tensor(w_lo[:, :], w_raw[:, :], w_hi[:, :], ALU.subtract).then_inc(dve_consts, 1)
            dve.wait_ge(u_loaded, 16)
            dve.tensor_scalar(u_half[:, :], u_raw[:, :], 0.5, None, ALU.mult).then_inc(dve_consts, 1)
            dve.wait_ge(pool_consts, 7)
            dve.tensor_scalar(rows[:, :, D:D + 1], toknum_i[:, :].unsqueeze(2), -FAR, None, ALU.add)
            dve.tensor_copy(expert_no[:, :, :, :], expert_i[:, :, :, :])
            dve.tensor_copy(group0[:, :, :], group0_i[:, :, :])
            dve.memset(eps[:, :], EPS)
            dve.memset(cnt[:, :, :, :], 0.0).then_inc(dve_consts, 1)
            dve.wait_ge(dve_consts, 4)

            def root(i, n):
                a, m = (slice(None), i % 2, slice(0, T)), moments[i % 2]
                x, y, p, b = root_x[a], root_y[a], root_p[a], root_b[a]
                if n:
                    dve.wait_ge(root_step, RT * i + n)
                if n == 0:
                    ins = dve.tensor_scalar(x, m[:, :, 1], EPS, None, ALU.add)
                elif n == 1:
                    ins = dve.tensor_scalar(y.bitcast(I32), x.bitcast(I32), -0.5, float(0x5f3759df), ALU.mult, ALU.add)
                elif n == RT - 1:
                    ins = dve.scalar_tensor_tensor(out=b, in0=m[:, :, 0], scalar=-1.0, in1=y, op0=ALU.mult, op1=ALU.mult)
                elif n % 3 == 2:
                    ins = dve.tensor_tensor(p, y, y, ALU.mult)
                elif n % 3 == 0:
                    ins = dve.scalar_tensor_tensor(out=p, in0=p, scalar=-0.5, in1=x, op0=ALU.mult, op1=ALU.mult)
                else:
                    ins = dve.scalar_tensor_tensor(out=y, in0=p, scalar=1.5, in1=y, op0=ALU.add, op1=ALU.mult)
                ins.then_inc(root_step, 1)

            def roots(s, first, last):
                if 0 <= s - 1 < S:
                    for n in range(first, last):
                        root(s - 1, n)

            def sum_h(s):
                if 0 <= s < S:
                    dve.wait_ge(ht_ready, s + 1)
                    if s >= 2:
                        dve.wait_ge(xn_ready, T * (s - 1))
                    dve.scalar_tensor_tensor(out=y_sb[s % 2][:, :, :], in0=b_ht[:, :].rearrange("p (t d) -> p t d", t=T), scalar=0.5,
                                             in1=x_sb[s][:, :, :], op0=ALU.mult, op1=ALU.add).then_inc(y_ready, 1)

            def stat(s, t):
                if 0 <= s < S:
                    dve.wait_ge(y_ready, s + 1)
                    dve.bn_stats(stats[:, t, :], y_sb[s % 2][:, t, :]).then_inc(stats_ready, 1)

            def moment(s):
                if 0 <= s < S:
                    for t in range(T):
                        dve.wait_ge(stats_ready, T * s + t + 1)
                        ins = dve.bn_aggr(moments[s % 2][:, t, :], stats[:, t, :])
                    ins.then_inc(mom_ready, 1)
                    dve.wait_ge(mom_ready, s + 1)

            def statistics(s, i):
                if i == 0:
                    sum_h(s)
                elif i <= T:
                    stat(s, i - 1)
                else:
                    moment(s)

            def choose(b, between):
                k = 5 * b
                dve.wait_ge(logits_ready, GB * (b + 1))
                for t in range(BT):
                    dve.max(top[:, t, :], lg_ps[:, t, :]).then_inc(top_ready, 1)
                dve.wait_ge(top_ready, (BT + 1) * b + BT)
                dve.tensor_tensor(less[:, :, :], top[:, :, :], top[:, :, 0:1].broadcast_to([P, BT, E]), ALU.subtract).then_inc(top_ready, 1)
                for t in range(BT):
                    ins = dve.max_index(top_ix[:, t, :], top[:, t, :], lg_ps[:, t, :])
                ins.then_inc(topix_ready, 1)
                between(0)
                dve.wait_ge(exp_ready, b + 1)
                dve.tensor_reduce(total[:, :], ex[:, :, :], AX.X, ALU.add).then_inc(gates_step, 1)
                between(1)
                dve.wait_ge(gates_step, k + 1)
                dve.reciprocal(rtotal[:, :], total[:, :]).then_inc(gates_step, 1)
                between(2)
                dve.wait_ge(gates_step, k + 2)
                dve.tensor_tensor(gates[:, :, :], ex[:, :, 0:2], rtotal[:, :].unsqueeze(2).broadcast_to([P, BT, 2]), ALU.mult).then_inc(gates_step, 1)
                between(3)
                dve.wait_ge(gates_step, k + 3)
                dve.wait_ge(topix_ready, b + 1)
                dve.scalar_tensor_tensor(out=choice[:, :, :], in0=gates[:, :, :], scalar=0.0, in1=top_ix[:, :, 0:2],
                                         op0=ALU.is_gt, op1=ALU.mult).then_inc(gates_step, 1)
                between(4)
                dve.wait_ge(gates_step, k + 4)
                dve.tensor_tensor(chosen[:, :, :, :], expert_no[:, :, :, :], choice[:, :, :].unsqueeze(3).broadcast_to([P, BT, 2, E]),
                                  ALU.is_equal).then_inc(chosen_ready, 1)
                dve.scalar_tensor_tensor(out=base[:, :, :], in0=choice[:, :, :], scalar=float(C), in1=group0[:, :, :],
                                         op0=ALU.mult, op1=ALU.add).then_inc(base_step, 1)
                dve.tensor_scalar(void[:, :, :], gates[:, :, :], 0.0, FAR, ALU.is_equal, ALU.mult).then_inc(base_step, 1)
                between(5)
                dve.wait_ge(base_step, 3 * b + 2)
                dve.scalar_tensor_tensor(out=base[:, :, :], in0=base[:, :, :], scalar=float(b * GB * E * C), in1=void[:, :, :],
                                         op0=ALU.add, op1=ALU.add).then_inc(base_step, 1)
                dve.wait_ge(chosen_ready, b + 1)
                dve.tensor_tensor(gate_rows[:, :, :, :], chosen[:, :, :, :], gates[:, :, :].unsqueeze(3).broadcast_to([P, BT, 2, E]),
                                  ALU.mult).then_inc(gates_step, 1)

            def assign(s, n):
                if s >= 4 and s % 2 == 0:
                    assign_batch(s // 2 - 2, n)

            def assign_batch(b, n):
                if n == 0:
                    dve.wait_ge(places_ready, b + 1)
                    ins = dve.tensor_scalar(cnt[:, :, 1, :], cn_ps, float(C), None, ALU.min)
                else:
                    dve.wait_ge(slot_step, AS * b + n)
                if n == 1:
                    for g in range(GB):
                        ins = dve.tensor_tensor(place[:, g * T:(g + 1) * T, :, :], pl_ps[:, g * T:(g + 1) * T, :, :],
                                                cnt[:, g:g + 1, :, :].broadcast_to([P, T, 2, E]), ALU.add)
                elif n == 2:
                    ins = dve.tensor_tensor(place[:, :, :, :], place[:, :, :, :], chosen[:, :, :, :], ALU.mult)
                elif n == 3:
                    ins = dve.tensor_reduce(pos[:, :, :], place[:, :, :, :], AX.X, ALU.add)
                elif n == 4:
                    dve.wait_ge(base_step, 3 * (b + 1))
                    dve.tensor_scalar(over[:, :, :], pos[:, :, :], float(C), FAR, ALU.is_ge, ALU.mult)
                    ins = dve.tensor_tensor(pos[:, :, :], pos[:, :, :], base[:, :, :], ALU.add)
                elif n == 5:
                    ins = dve.tensor_tensor(slot_ix[b][:, :].rearrange("p (t c) -> p t c", c=2), pos[:, :, :], over[:, :, :], ALU.add)
                ins.then_inc(slot_step, 1)

            def gate_row(b):
                dve.wait_ge(gates_step, 5 * (b + 1))
                dve.tensor_tensor(rows[:, b * BT:(b + 1) * BT, D + 1:ROW], gate_rows[:, :, 0, :], gate_rows[:, :, 1, :], ALU.add).then_inc(gate_rows_in, 1)

            for s in range(S):
                if s >= 4 and s % 2 == 0:
                    choose(s // 2 - 2, lambda i: statistics(s - 1, i))
                else:
                    sum_h(s - 1)
                    for t in range(T):
                        stat(s - 1, t)
                    moment(s - 1)
                roots(s, 0, 2)
                if 1 <= s < S:
                    dve.wait_ge(gate_read, gate_no(s, 0))
                    dve.scalar_tensor_tensor(out=term_f[:, :], in0=act_g[0][:, :], scalar=1.0, in1=cell2[:, :],
                                             op0=ALU.add, op1=ALU.mult).then_inc(terms_ready, 1)
                roots(s, 2, 3)
                assign(s, 0)
                roots(s, 3, 4)
                assign(s, 1)
                if s < S:
                    dve.wait_ge(gate_read, gate_no(s, 2))
                    ins = dve.scalar_tensor_tensor(out=term_i[:, :] if s else cell2[:, :], in0=act_g[1][:, :], scalar=1.0,
                                                   in1=act_g[2][:, :], op0=ALU.add, op1=ALU.mult)
                    ins.then_inc(terms_ready if s else cell_ready, 1)
                roots(s, 4, 5)
                if s == 0:
                    low_x(1)
                if 1 <= s < S:
                    dve.wait_ge(terms_ready, 2 * s)
                    dve.scalar_tensor_tensor(out=cell2[:, :], in0=term_f[:, :], scalar=0.5, in1=term_i[:, :],
                                             op0=ALU.mult, op1=ALU.add).then_inc(cell_ready, 1)
                roots(s, 5, 6)
                assign(s, 2)
                roots(s, 6, 7)
                assign(s, 3)
                roots(s, 7, 8)
                if s < S:
                    dve.wait_ge(tanh_ready, s + 1)
                    dve.wait_ge(gate_read, gate_no(s, 3))
                    dve.scalar_tensor_tensor(out=h2[:, :], in0=act_g[3][:, :], scalar=1.0, in1=tanh_c[:, :],
                                             op0=ALU.add, op1=ALU.mult).then_inc(h_ready, 1)
                roots(s, 8, 9)
                assign(s, 4)
                roots(s, 9, 10)
                assign(s, 5)
                roots(s, 10, 11)
                roots(s, 11, RT)
                if s + 2 < S:
                    low_x(s + 2)
                if s >= 4 and s % 2 == 0:
                    gate_row(s // 2 - 2)

            def low_xd(u):
                dve.wait_ge(xdhi_ready, u + 1)
                w = width(u)
                dve.tensor_tensor(xdt_lo[u % 2][:, 0:w], b_xt[:, 0:w], xdt_hi[u % 2][:, 0:w], ALU.subtract).then_inc(xdlo_ready, 1)

            def low_hid(u, k):
                n = u * NCH + k
                m = P if k < FULL else P // 2
                dve.wait_ge(hidhi_ready, n + 1)
                w = width(u)
                low = hid_lo[n % RH][:, 0:w] if k < FULL else hid_hi[n % RH][P // 2:P, 0:w]
                dve.tensor_tensor(low, hid[n % RH][0:m, 0:w], hid_hi[n % RH][0:m, 0:w], ALU.subtract).then_inc(hidlo_ready, 1)

            def give(u):
                e, ng = expert(u), len(groups(u))
                dve.wait_ge(eo_ready, u + 1)
                if u >= CR:
                    for g in groups(u - CR):
                        dve.wait_ge(added[g], 16 * adds(g, u - CR + 1))
                dve.tensor_tensor(contrib[u % CR][:, 0:ng, :], y_rows(u).rearrange("p (g d) -> p g d", g=ng),
                                  xd[u % 4][:, 0:ng, D + 1 + e:D + 2 + e].broadcast_to([P, ng, D]), ALU.mult).then_inc(contrib_ready, 1)
                dve.tensor_scalar(token_ix[u % CR][:, 0:ng], xd[u % 4][:, 0:ng, D], FAR, None, ALU.add).then_inc(contrib_ready, 1)

            def chunk(u, k):
                n, w = u * NCH + k, width(u)
                m = P if k < FULL else P // 2
                dve.wait_ge(gelu_ready, n + 1)
                dve.wait_ge(pre_ready, (2 * FULL + 1) * u + min(2 * k + 2, 2 * FULL + 1))
                dve.tensor_tensor(hid[n % RH][0:m, 0:w], act0[n % RH][0:m, 0:w], pre(n, P)[1], ALU.mult).then_inc(hid_ready, 1)
                if k >= 1:
                    low_hid(u, k - 1)
                elif u >= 1:
                    low_hid(u - 1, NCH - 1)
                if k == 3 and u + 1 < NU:
                    low_xd(u + 1)
                if k == NCH - 1 and u >= 1:
                    give(u - 1)

            def fin_stat(n):
                g, t = divmod(n, T)
                dve.wait_ge(fin_in[g], 16)
                dve.bn_stats(fin_stats[:, n, :], fin[g][:, t, :]).then_inc(fstats_ready, 1)

            def fin_moment(n):
                dve.wait_ge(fstats_ready, n + 1)
                dve.bn_aggr(fin_mom[:, n, :], fin_stats[:, n, :]).then_inc(fmom_ready, 1)

            low_xd(0)
            def statistics_and_chunk(i):
                statistics(S - 1, i)
                if i in (2, 4):
                    chunk(0, i // 2 - 1)

            choose(NB - 2, statistics_and_chunk)
            for n in range(RT):
                root(S - 1, n)
                if n < AS:
                    assign_batch(NB - 2, n)
                if n % 4 == 1:
                    chunk(0, n // 4 + 2)
            gate_row(NB - 2)
            chunk(0, NCH - 1)
            for k in range(NCH):
                chunk(1, k)
            among = {0: (2, 0), 2: (2, 1), 4: (2, 2)}
            choose(NB - 1, lambda i: chunk(*among[i]) if i in among else None)
            for k in range(3, NCH):
                chunk(2, k)
                assign_batch(NB - 1, 2 * (k - 3))
                assign_batch(NB - 1, 2 * (k - 3) + 1)
            gate_row(NB - 1)
            for u in range(3, NU):
                for k in range(NCH):
                    chunk(u, k)
                    for n, at in enumerate(early):
                        if at == (u, k):
                            fin_stat(n)
            low_hid(NU - 1, NCH - 1)

            def fin_argument(i):
                c = fin_cols[i]
                dve.wait_ge(fmom_ready, c.stop)
                dve.tensor_scalar(root_x[:, 1, c], fin_mom[:, c, 1], EPS, None, ALU.add).then_inc(fx_ready, 1)

            def fin_root_step(i, n):
                a = (slice(None), 1, fin_cols[i])
                x, y, p, b = root_x[a], root_y[a], root_p[a], root_b[a]
                if n:
                    dve.wait_ge(froot_step, FT * i + n)
                if n == 0:
                    dve.wait_ge(fsqrt_ready, i + 1)
                    ins = dve.reciprocal(y, root_p[:, 0, fin_cols[i]])
                elif n == 1:
                    ins = dve.tensor_tensor(p, y, y, ALU.mult)
                elif n == 2:
                    dve.wait_ge(fx_ready, i + 1)
                    ins = dve.scalar_tensor_tensor(out=p, in0=p, scalar=-0.5, in1=x, op0=ALU.mult, op1=ALU.mult)
                elif n == 3:
                    ins = dve.scalar_tensor_tensor(out=y, in0=p, scalar=1.5, in1=y, op0=ALU.add, op1=ALU.mult)
                else:
                    ins = dve.scalar_tensor_tensor(out=b, in0=fin_mom[:, fin_cols[i], 0], scalar=-1.0, in1=y, op0=ALU.mult, op1=ALU.mult)
                ins.then_inc(froot_step, 1)

            def fin_rows(g):
                for t in range(T):
                    if fin_who[g][t] == "v":
                        fin_row_by_mean(dve, g, t)

            for n in range(len(early), HALF * T):
                fin_stat(n)
            give(NU - 1)
            for n in range(HALF * T):
                fin_moment(n)
            fin_argument(0)
            for n in range(FT):
                fin_root_step(0, n)
            for g in range(HALF):
                fin_rows(g)
            for i in range(1, FR):
                c = fin_cols[i]
                for j, n in enumerate(range(c.start, c.stop)):
                    fin_stat(n)
                    if i >= 2 and j < FT:
                        fin_root_step(i - 1, j)
                    if j % T == T - 1:
                        for m in range(n - T + 1, n + 1):
                            fin_moment(m)
                fin_argument(i)
                if i >= 2:
                    for g in range(HALF + GB * (i - 2), HALF + GB * (i - 1)):
                        fin_rows(g)
            for n in range(FT):
                fin_root_step(FR - 1, n)
            for g in range(S - GB, S):
                fin_rows(g)


_INS = ['L0_attn_input_seq', 'L0_attn_w', 'L0_attn_u', 'L0_attn_bias', 'L0_ffn_router_w', 'L0_ffn_w0_kernel',
        'L0_ffn_w1_kernel', 'L0_ffn_wo_kernel']


def kernel(**inputs):
    import numpy as np
    import concourse.bacc as bacc
    from concourse import mybir as mb
    from concourse.bass_utils import run_bass_kernel_spmd as run

    nc = bacc.Bacc("TRN2", target_bir_lowering=False, num_devices=1)
    arrays, args = {}, []
    for name in _INS:
        a = np.ascontiguousarray(inputs[name])
        arrays[f"in_{name}_dram"] = a
        args.append(nc.dram_tensor(f"in_{name}_dram", a.shape, mb.dt.from_np(a.dtype), kind="ExternalInput").ap())
    shape = inputs['L0_attn_input_seq'].shape
    out = nc.dram_tensor("out_0_dram", shape, mb.dt.float32, kind="ExternalOutput").ap()
    build(nc, *args, out)
    r = run(nc, [arrays], core_ids=[0])
    return r.results[0]["out_0_dram"]
```
